# Optimizing a Trainium2 kernel written in Bass

```python
import numpy as np
import jax
import jax.numpy as jnp

def _softmax(x, axis=-1):
    return jax.nn.softmax(x, axis=axis)

def _gelu(x):
    return jax.nn.gelu(x, approximate=True)

def _silu(x):
    return jax.nn.silu(x)

def _sigmoid(x):
    return jax.nn.sigmoid(x)

def _layernorm(x, axis=-1, eps=1e-05):
    m = jnp.mean(x, axis=axis, keepdims=True)
    v = jnp.var(x, axis=axis, keepdims=True)
    return (x - m) / jnp.sqrt(v + eps)

def _scatter_add(tgt, idx, src, axis=0):
    return tgt.at[idx].add(src)

def _segment_sum(src, seg, n):
    return jax.ops.segment_sum(src, seg, n)
kernel_name = 'mk_gps_d1_gnn_r8_e35992'

def setup_inputs(seed: int=0):
    np.random.seed(seed)
    _w = jnp.asarray

    def _rec_inputs():
        import jax
        import jax.numpy as jnp
        _gk = jax.random.key(seed)
        x = -0.0003713 + 1 * jax.random.normal(jax.random.fold_in(_gk, 1), (6250, 256), jnp.float32)
        src = jax.random.randint(jax.random.fold_in(_gk, 2), (100000,), 0, 6250, jnp.int32)
        dst = jnp.minimum((6250 * jax.random.uniform(jax.random.fold_in(_gk, 3), (100000,)) ** 2.0).astype(jnp.int32), 49999)
        _o = jnp.argsort(dst, stable=True)
        src = src[_o]
        dst = dst[_o]
        return (x, src, dst)
    x, src, dst = _rec_inputs()

    def _L0_gnn_setup():
        import jax, jax.numpy as jnp
        import numpy as np
        N_NODES = 6250
        N_EDGES = 100000
        IN_FEAT = 256
        OUT_FEAT = 64
        NHEAD = 4
        ALPHA = 0.2
        key = jax.random.key(seed)
        k_x, k_e, k_w, k_al, k_ar = jax.random.split(key, 5)
        x = jax.random.normal(k_x, (N_NODES, IN_FEAT), dtype=jnp.float32)
        edge = jax.random.randint(k_e, (2, N_EDGES), 0, N_NODES, dtype=jnp.int64)
        stdv_w = np.sqrt(6.0 / (IN_FEAT + OUT_FEAT * NHEAD))
        W = jax.random.uniform(k_w, (IN_FEAT, OUT_FEAT * NHEAD), minval=-stdv_w, maxval=stdv_w, dtype=jnp.float32)
        stdv_a = np.sqrt(6.0 / (NHEAD + OUT_FEAT))
        a_l = jax.random.uniform(k_al, (1, NHEAD, OUT_FEAT), minval=-stdv_a, maxval=stdv_a, dtype=jnp.float32)
        a_r = jax.random.uniform(k_ar, (1, NHEAD, OUT_FEAT), minval=-stdv_a, maxval=stdv_a, dtype=jnp.float32)
        return {'x': x, 'edge': edge, 'W': W, 'a_l': a_l, 'a_r': a_r}
    _L0_gnn_all = _L0_gnn_setup()
    _L0_gnn_in = {k: v for k, v in _L0_gnn_all.items() if k in ('W', 'a_l', 'a_r')}
    del _L0_gnn_all

    def _L0_mix_setup():
        import jax, jax.numpy as jnp
        import numpy as np
        HEADS = 8
        DIM_HEAD = 64
        EPS = 1e-05

        def _inst_norm_lastdim(t):
            mu = jnp.mean(t, axis=-1, keepdims=True)
            var = jnp.mean(jnp.square(t - mu), axis=-1, keepdims=True)
            return (t - mu) * jax.lax.rsqrt(var + EPS)
        key = jax.random.key(seed)
        k1, k2, k3, k4 = jax.random.split(key, 4)
        b, n, dim = (4, 1024, 256)
        inner = HEADS * DIM_HEAD
        x = jax.random.normal(k1, (b, n, dim), dtype=jnp.float32)
        Wqkv = jax.random.normal(k2, (3 * inner, dim), dtype=jnp.float32) * (1.0 / np.sqrt(dim))
        Wout = jax.random.normal(k3, (dim, inner), dtype=jnp.float32) * (1.0 / np.sqrt(inner))
        bout = jax.random.normal(k4, (dim,), dtype=jnp.float32) * 0.01
        return {'x': x, 'Wqkv': Wqkv, 'Wout': Wout, 'bout': bout}
    _L0_mix_all = _L0_mix_setup()
    _L0_mix_in = {k: v for k, v in _L0_mix_all.items() if k in ('Wqkv', 'Wout', 'bout')}
    del _L0_mix_all

    def _L0_ffn_setup():
        import jax, jax.numpy as jnp
        import numpy as np
        E = 8
        K = 2
        D = 256
        H = 512
        DOUT = 256
        EPS = 1e-05
        key = jax.random.key(seed)
        ks = jax.random.split(key, 9)
        s = 0.02
        return {'x': jax.random.normal(ks[0], (4, 1024, D), jnp.float32), 'gamma': 1.0 + 0.05 * jax.random.normal(ks[1], (D,), jnp.float32), 'beta': 0.05 * jax.random.normal(ks[2], (D,), jnp.float32), 'Wr': 0.01 * jax.random.normal(ks[3], (D, E), jnp.float32), 'br': jnp.zeros((E,), jnp.float32), 'W1': s * jax.random.normal(ks[4], (E, D, H), jnp.float32), 'b1': s * jax.random.normal(ks[5], (E, H), jnp.float32), 'W2': s * jax.random.normal(ks[6], (E, H, DOUT), jnp.float32), 'b2': s * jax.random.normal(ks[7], (E, DOUT), jnp.float32)}
    _L0_ffn_all = _L0_ffn_setup()
    _L0_ffn_in = {k: v for k, v in _L0_ffn_all.items() if k in ('gamma', 'beta', 'Wr', 'br', 'W1', 'b1', 'W2', 'b2')}
    del _L0_ffn_all
    return {'x': x, 'src': src, 'dst': dst, 'L0_gnn_W': _L0_gnn_in['W'], 'L0_gnn_a_l': _L0_gnn_in['a_l'], 'L0_gnn_a_r': _L0_gnn_in['a_r'], 'L0_mix_Wqkv': _L0_mix_in['Wqkv'], 'L0_mix_Wout': _L0_mix_in['Wout'], 'L0_mix_bout': _L0_mix_in['bout'], 'L0_ffn_gamma': _L0_ffn_in['gamma'], 'L0_ffn_beta': _L0_ffn_in['beta'], 'L0_ffn_Wr': _L0_ffn_in['Wr'], 'L0_ffn_br': _L0_ffn_in['br'], 'L0_ffn_W1': _L0_ffn_in['W1'], 'L0_ffn_b1': _L0_ffn_in['b1'], 'L0_ffn_W2': _L0_ffn_in['W2'], 'L0_ffn_b2': _L0_ffn_in['b2']}

def reference(x, src, dst, L0_gnn_W, L0_gnn_a_l, L0_gnn_a_r, L0_mix_Wqkv, L0_mix_Wout, L0_mix_bout, L0_ffn_gamma, L0_ffn_beta, L0_ffn_Wr, L0_ffn_br, L0_ffn_W1, L0_ffn_b1, L0_ffn_W2, L0_ffn_b2):
    import jax
    import jax.numpy as jnp

    def _L0_gnn_ref(x, edge, W, a_l, a_r):
        import jax, jax.numpy as jnp
        import numpy as np
        N_NODES = 6250
        N_EDGES = 100000
        IN_FEAT = 256
        OUT_FEAT = 64
        NHEAD = 4
        ALPHA = 0.2
        N = x.shape[0]
        H, F = (a_l.shape[1], a_l.shape[2])
        h = (x @ W).reshape(N, H, F)
        h_l = (a_l * h).sum(-1)
        h_r = (a_r * h).sum(-1)
        row, col = (edge[0], edge[1])
        e = jax.nn.leaky_relu(h_l[row] + h_r[col], ALPHA)
        m = jax.lax.stop_gradient(jax.ops.segment_max(e, row, num_segments=N))
        ex = jnp.exp(e - m[row])
        denom = jax.ops.segment_sum(ex, row, num_segments=N)[row]
        att = ex / jnp.maximum(denom, jnp.asarray(1e-16, ex.dtype))
        msg = att[:, :, None] * h[col]
        out = jax.ops.segment_sum(msg, row, num_segments=N)
        return out.reshape(N, H * F)

    def _L0_mix_ref(x, Wqkv, Wout, bout):
        import jax, jax.numpy as jnp
        import numpy as np
        HEADS = 8
        DIM_HEAD = 64
        EPS = 1e-05

        def _inst_norm_lastdim(t):
            mu = jnp.mean(t, axis=-1, keepdims=True)
            var = jnp.mean(jnp.square(t - mu), axis=-1, keepdims=True)
            return (t - mu) * jax.lax.rsqrt(var + EPS)
        b, n, dim = x.shape
        qkv = jnp.einsum('bnc,fc->bnf', x, Wqkv)
        q, k, v = jnp.split(qkv, 3, axis=-1)

        def to_heads(t):
            return t.reshape(b, n, HEADS, DIM_HEAD).transpose(0, 2, 1, 3)
        q, k, v = (to_heads(q), to_heads(k), to_heads(v))
        k = _inst_norm_lastdim(k)
        v = _inst_norm_lastdim(v)
        dots = jnp.einsum('bhnd,bhne->bhde', k, v)
        out = jnp.einsum('bhnd,bhde->bhne', q, dots) / n
        out = out.transpose(0, 2, 1, 3).reshape(b, n, HEADS * DIM_HEAD)
        return jnp.einsum('bnf,cf->bnc', out, Wout) + bout

    def _L0_ffn_ref(x, gamma, beta, Wr, br, W1, b1, W2, b2):
        import jax, jax.numpy as jnp
        import numpy as np
        E = 8
        K = 2
        D = 256
        H = 512
        DOUT = 256
        EPS = 1e-05
        mu = jnp.mean(x, axis=-1, keepdims=True)
        var = jnp.mean(jnp.square(x - mu), axis=-1, keepdims=True)
        xn = (x - mu) * jax.lax.rsqrt(var + EPS) * gamma + beta
        logits = jnp.einsum('bsd,de->bse', xn, Wr) + br
        top_vals, top_idx = jax.lax.top_k(logits, K)
        w = jax.nn.softmax(top_vals, axis=-1)
        w_full = jnp.einsum('bsk,bske->bse', w, jax.nn.one_hot(top_idx, E, dtype=w.dtype))
        y = jnp.zeros(x.shape[:-1] + (DOUT,), x.dtype)
        for e in range(E):
            h = jax.nn.gelu(jnp.einsum('bsd,dh->bsh', xn, W1[e]) + b1[e], approximate=False)
            y_e = jnp.einsum('bsh,hd->bsd', h, W2[e]) + b2[e]
            y = y + y_e * w_full[..., e, None]
        return y
    edge_index = jnp.stack([src, dst])
    xn = _layernorm(x, axis=-1)
    x = x + _L0_gnn_ref(xn, edge_index, L0_gnn_W, L0_gnn_a_l, L0_gnn_a_r) + _L0_mix_ref(xn[None], L0_mix_Wqkv, L0_mix_Wout, L0_mix_bout)[0]
    x = x + _L0_ffn_ref(_layernorm(x, axis=-1)[None], L0_ffn_gamma, L0_ffn_beta, L0_ffn_Wr, L0_ffn_br, L0_ffn_W1, L0_ffn_b1, L0_ffn_W2, L0_ffn_b2)[0]
    return x

_drawn_inputs = setup_inputs


def setup_inputs(seed=0):
    import zlib

    import numpy as np

    out = dict(_drawn_inputs(seed))
    spreads = {'L0_ffn_br': (0.0, 0.1)}
    factors = {'L0_mix_bout': 7.201,
     'L0_ffn_gamma': 7.103,
     'L0_ffn_beta': 5.737,
     'L0_ffn_b1': 8.0,
     'L0_ffn_b2': 5.071}
    for name, (base, spread) in spreads.items():
        noise = np.random.default_rng([zlib.crc32(name.encode()), seed]).standard_normal(out[name].shape)
        drawn = base * np.exp(spread * noise) if base else spread * noise
        out[name] = jnp.asarray(drawn.astype(out[name].dtype))
    for name, factor in factors.items():
        out[name] = (out[name] * factor).astype(out[name].dtype)
    return out
```

```python
from contextlib import ExitStack

import concourse.bass as bass
from concourse import mybir
from concourse.alu_op_type import AluOpType as ALU

F32, I32, U32, BF16 = mybir.dt.float32, mybir.dt.int32, mybir.dt.uint32, mybir.dt.bfloat16
ACT = mybir.ActivationFunctionType
AX = mybir.AxisListType
ds = bass.ds

N, D = 6250, 256
EDGES = 100000
GH, GF = 4, 64
SLOPE = 0.2
MH, MF = 8, 64
INNER = MH * MF
NE, HID = 8, 512
EPS = 1e-5
TP, NT = 125, 50
EC = EDGES // TP
EK = EC // NT
HALF = EC // 2
HK = 20
BR = 32
NB = -(-N // BR)
HI, LO = -(-NB // 16), 16
NBT = NB // 2
GU = 4
RING = 6
NCH = -(-((EDGES + NB * 128) // 128) // (GU * RING)) * GU * RING
NG = NCH // GU
HW = GF + 1
TW = GH * HW
ROW = TW + GH
BIG, FLOOR = 1e30, 1e28
COLBITS = 13
PAD = BR << COLBITS
TB = 5
NBL = NT // TB
CAP = N + 128
MC = -(-((2 * N + NE * 127) // 128) // 2) * 2
C_ID, C_LT, C_IO = 0, 128, 256
CW = C_IO + NCH


def constants():
    import numpy as np
    c = np.zeros((128, CW), np.float32)
    p = np.arange(128)
    c[:, C_ID:C_ID + 128] = np.eye(128)
    c[:, C_LT:C_LT + 128] = p[:, None] < p[None, :]
    c[:, C_IO:] = np.arange(NCH)
    return c


def bc(ap, shape):
    return ap.to_broadcast(shape)


def after(eng, g, sem, value):
    eng.wait_ge(sem, value)
    eng.sem_inc(g.passed, 1)


class Parts:

    def __init__(self, nc, ctx, stage):
        self.nc, self.ctx, self.stage, self.sems_held = nc, ctx, stage, []
        ctx.callback(self.clear)

    def clear(self):
        if self.sems_held:
            self.nc.clear_and_free_semaphores(self.sems_held)
            self.nc.all_engine_barrier()

    def sb(self, name, shape, dt=F32):
        return self.ctx.enter_context(self.nc.sbuf_tensor(f"{self.stage}_{name}", shape, dt))

    def sem(self, name):
        self.sems_held.append(self.nc.alloc_semaphore(name=f"{self.stage}_{name}"))
        return self.sems_held[-1]

    def sems(self, name, n):
        return [self.sem(f"{name}{k}") for k in range(n)]


def setup(nc, g):
    with ExitStack() as ctx:
        t = Parts(nc, ctx, "setup")
        sb, sem = t.sb, t.sem
        room = g.xnT[0:TP, :, :, :].rearrange("p t q n -> p (t q n)")
        hif, lof, *ints = (room[:, n * EC:(n + 1) * EC] for n in range(8))
        srcs, dsts, bkti, hii, loi, pk1 = (r.bitcast(I32) for r in ints)
        oneh = sb("oneh", [TP, 2, HK, HI + LO], BF16)
        zerob = sb("zerob", [TP, HI + LO], BF16)
        hists = sb("hists", [HI, 2, LO])
        cnt = sb("cnt", [128, 2, HI * LO])
        tot, toti = sb("tot", [128, NB]), sb("toti", [128, NB], I32)
        totj, chk = sb("totj", [128, NB], I32), sb("chk", [128, NB])
        zero, endc, firstc = sb("zero", [128, NB]), sb("endc", [128, NB]), sb("firstc", [128, NB])
        padt = sb("padt", [128, NCH], I32)
        zhl = sb("zhl", [NB * BR - N, GH])
        abc = sb("abc", [128, 2, D])
        wprod = sb("wprod", [128, 2, 2, D])
        wkvn = sb("wkvn", [128, 8, D])
        wmean = sb("wmean", [128, 2, 2 * MH])
        won = sb("won", [128, 2, INNER])

        const_in, edge_in, w_in, a_in = sem("const_in"), sem("edge_in"), sem("w_in"), sem("a_in")
        kv_in, wo_in = sem("kv_in"), sem("wo_in")
        ones_ready, cast_ready = sem("ones_ready"), sem("cast_ready")
        ints_ready, digit_ready = sem("ints_ready"), sem("digit_ready")
        fill_ready = sem("fill_ready")
        oneh_ready, oneh_used = sem("oneh_ready"), sem("oneh_used")
        hist_done, hist_copied, hist_out, cnt_in = (sem("hist_done"), sem("hist_copied"),
                                                    sem("hist_out"), sem("cnt_in"))
        step, cols_ready, cols_out = sem("table_step"), sem("cols_ready"), sem("cols_out")
        wt_done, wt_copied = sem("wt_done"), sem("wt_copied")
        mean_ready, prod_ready, a_ready = sem("mean_ready"), sem("prod_ready"), sem("a_ready")
        block = ctx.enter_context(nc.Block())
        b = g.bank

        @block.sync
        def _(sp):
            sp.dma_start(g.cst[:, :], g.const).then_inc(const_in, 16)
            sp.dma_start(srcs[:, :], g.src.rearrange("(p c) -> p c", p=TP)).then_inc(edge_in, 16)
            sp.dma_start(dsts[:, :], g.dst.rearrange("(p c) -> p c", p=TP)).then_inc(edge_in, 16)
            sp.dma_start(wkvn[:, :, :], g.wqkv[INNER:3 * INNER, :].rearrange("(s p) c -> p s c", p=128)).then_inc(kv_in, 16)
            sp.dma_start(won[:, :, :], g.wout.rearrange("(s p) f -> p s f", p=128)).then_inc(wo_in, 16)
            sp.dma_start(g.wa[:, :, 0:D], g.gW.rearrange("(k p) f -> p k f", p=128)).then_inc(w_in, 16)
            sp.dma_start(abc[:, 0, :], g.gar.rearrange("a h f -> a (h f)").partition_broadcast(128)).then_inc(a_in, 16)
            sp.dma_start(abc[:, 1, :], g.gal.rearrange("a h f -> a (h f)").partition_broadcast(128)).then_inc(a_in, 16)
            sp.dma_start(g.wq[:, :, :], g.wqkv[0:INNER, :].rearrange("(s p) c -> p s c", p=128)).then_inc(g.late_in, 16)
            sp.dma_start(g.wrs[:, :, :], g.wr.rearrange("(k p) e -> p k e", p=128)).then_inc(g.late_in, 16)
            sp.dma_start(g.rows[0:1, 0:D], g.bout.rearrange("(a f) -> a f", a=1)).then_inc(g.late_in, 16)
            sp.dma_start(g.rows[0:1, D:D + NE], g.br.rearrange("(a f) -> a f", a=1)).then_inc(g.late_in, 16)
            for e in range(NE):
                sp.dma_start(g.w1s[:, e, :, :], g.w1[e].rearrange("(k p) h -> p k h", p=128)).then_inc(g.late_in, 16)
                sp.dma_start(g.w2s[:, e, :, :], g.w2[e].rearrange("(k p) h -> p k h", p=128)).then_inc(g.late_in, 16)
            sp.wait_ge(fill_ready, 2)
            sp.dma_start(g.sorted_d.rearrange("(p c) a -> p (c a)", p=128), padt[:, :]).then_inc(g.filled, 16)
            sp.dma_start(g.hl_d[N:NB * BR, :], zhl[:, :]).then_inc(g.filled, 16)
            sp.wait_ge(hist_copied, 2)
            sp.dma_start(g.hist_d.rearrange("s (h l) -> h s l", l=LO), hists[:, :, :]).then_inc(hist_out, 16)
            sp.wait_ge(hist_out, 16)
            sp.dma_start(cnt[:, :, :], g.hist_d.rearrange("s b -> (s b)").partition_broadcast(128).rearrange("p (s b) -> p s b", s=2)).then_inc(cnt_in, 16)
            sp.wait_ge(cols_ready, 2)
            sp.dma_start(g.cols_d[0:1, :], firstc[0:1, :]).then_inc(cols_out, 16)
            sp.dma_start(g.cols_d[1:2, :], endc[0:1, :]).then_inc(cols_out, 16)
            sp.wait_ge(cols_out, 32)
            sp.wait_ge(g.filled, 32)
            sp.wait_ge(g.late_in, 16 * (4 + 2 * NE))

        @block.gpsimd
        def _(pool):
            pool.memset(padt[:, :], PAD).then_inc(fill_ready, 1)
            pool.memset(zhl[:, :], 0.0).then_inc(fill_ready, 1)

        @block.vector
        def _(v):
            v.memset(g.ones[:, :], 1.0).then_inc(ones_ready, 1)
            v.memset(zerob[:, :], 0.0).then_inc(ones_ready, 1)
            v.memset(zero[:, :], 0.0)
            v.memset(g.eps[:, :], EPS)
            v.memset(g.zero[:, :], 0.0).then_inc(ones_ready, 1)
            v.wait_ge(edge_in, 32)
            v.tensor_scalar(bkti[:, :], srcs[:, :], 5, None, ALU.arith_shift_right).then_inc(ints_ready, 1)
            v.tensor_scalar(hii[:, :], srcs[:, :], 9, None, ALU.arith_shift_right).then_inc(ints_ready, 1)
            v.tensor_scalar(loi[:, :], srcs[:, :], 5, LO - 1, ALU.arith_shift_right, ALU.bitwise_and).then_inc(ints_ready, 1)
            v.tensor_scalar(pk1[:, :], srcs[:, :], BR - 1, COLBITS, ALU.bitwise_and, ALU.logical_shift_left).then_inc(ints_ready, 1)
            v.wait_ge(ints_ready, 4)
            v.tensor_copy(hif[:, :], hii[:, :]).then_inc(digit_ready, 1)
            v.tensor_copy(lof[:, :], loi[:, :]).then_inc(digit_ready, 1)
            v.tensor_copy(g.bktf[:, :], bkti[:, :])
            v.tensor_tensor(g.packi[:, :], pk1[:, :], dsts[:, :], ALU.bitwise_or)
            v.wait_ge(const_in, 16)
            v.wait_ge(digit_ready, 2)
            iota = g.iota[0:TP, :]

            def digits(j, first):
                for k in range(2):
                    if not first:
                        v.wait_ge(oneh_used, 2 * j + k - 1)
                    c0 = (2 * j + k) * HK
                    v.tensor_tensor(oneh[:, k, :, 0:HI], bc(hif[:, ds(c0, HK)].unsqueeze(2), [TP, HK, HI]),
                                    bc(iota[:, 0:HI].unsqueeze(1), [TP, HK, HI]), ALU.is_equal).then_inc(oneh_ready, 1)
                    v.tensor_tensor(oneh[:, k, :, HI:HI + LO], bc(lof[:, ds(c0, HK)].unsqueeze(2), [TP, HK, LO]),
                                    bc(iota[:, 0:LO].unsqueeze(1), [TP, HK, LO]), ALU.is_equal).then_inc(oneh_ready, 1)
            digits(0, True)
            with v.Fori(1, EC // HK // 2) as j:
                digits(j, False)
            v.tensor_copy(g.ltb[:, :], g.cst[:, C_LT:C_LT + 128])
            v.tensor_scalar(g.geb[:, :], g.cst[:, C_LT:C_LT + 128], -1.0, 1.0, ALU.mult, ALU.add)
            v.tensor_copy(g.iotab[:, :], g.iota[:, 0:NB])
            v.wait_ge(hist_done, 2)
            for s in range(2):
                v.tensor_copy(hists[:, s, :], b[s][0:HI, 0:LO]).then_inc(hist_copied, 1)
            v.wait_ge(w_in, 16)
            v.wait_ge(a_in, 32)
            for k in range(2):
                for s in range(2):
                    v.tensor_tensor(wprod[:, k, s, :], g.wa[:, k, 0:D], abc[:, s, :], ALU.mult).then_inc(prod_ready, 1)
            v.wait_ge(prod_ready, 4)
            for k in range(2):
                for s in range(2):
                    v.tensor_reduce(g.wa[:, k, D + s * GH:D + (s + 1) * GH],
                                    wprod[:, k, s, :].rearrange("p (h f) -> p h f", h=GH), axis=AX.X, op=ALU.add)
            n = [0]

            def link(ins):
                n[0] += 1
                ins.then_inc(step, 1)
                v.wait_ge(step, n[0])
            v.wait_ge(cnt_in, 16)
            link(v.tensor_tensor(tot[:, :], cnt[:, 0, 0:NB], cnt[:, 1, 0:NB], ALU.add))
            link(v.tensor_scalar(toti[:, :], tot[:, :], 127.0, None, ALU.add))
            link(v.tensor_scalar(totj[:, :], toti[:, :], 7, None, ALU.arith_shift_right))
            link(v.tensor_scalar(chk[:, :], totj[:, :], 1.0, None, ALU.max))
            v.tensor_tensor_scan(endc[:, :], chk[:, :], zero[:, :], 0.0, ALU.add, ALU.add).then_inc(cols_ready, 1)
            v.wait_ge(cols_ready, 1)
            v.tensor_tensor(firstc[:, :], endc[:, :], chk[:, :], ALU.subtract).then_inc(cols_ready, 1)
            v.wait_ge(cols_ready, 2)
            link(v.tensor_scalar(g.firsts[:, 0, :], firstc[:, :], 128.0, None, ALU.mult))
            link(v.tensor_tensor(g.firsts[:, 1, :], g.firsts[:, 0, :], cnt[:, 0, 0:NB], ALU.add))
            v.wait_ge(wt_copied, 6)
            for k in range(2):
                v.tensor_reduce(wmean[:, k, :], g.wkvT[:, k, :].rearrange("p (h f) -> p h f", f=MF),
                                axis=AX.X, op=ALU.add).then_inc(mean_ready, 1)
            v.wait_ge(mean_ready, 2)
            for k in range(2):
                w = g.wkvT[:, k, :].rearrange("p (h f) -> p h f", f=MF)
                v.scalar_tensor_tensor(w, bc(wmean[:, k, :].unsqueeze(2), [128, 2 * MH, MF]), -1.0 / MF, w,
                                       ALU.mult, ALU.add)

        @block.tensor
        def _(pe):
            pe.wait_ge(ones_ready, 2)
            for s in range(2):
                pe.matmul(b[s][0:HI, 0:LO], zerob[:, 0:HI], zerob[:, HI:HI + LO], start=True, stop=True)
            steps = EC // HK // 2
            for s in range(2):
                with pe.Fori(s * steps // 2, (s + 1) * steps // 2) as j:
                    for k in range(2):
                        pe.wait_ge(oneh_ready, 4 * j + 2 * k + 2)
                        for c in range(HK):
                            m = pe.matmul(b[s][0:HI, 0:LO], oneh[:, k, c, 0:HI], oneh[:, k, c, HI:HI + LO],
                                          start=False, stop=True, skip_group_check=True)
                        m.then_inc(oneh_used, 1)
            pe.matmul(b[0][0:HI, 0:LO], zerob[:, 0:HI], zerob[:, HI:HI + LO], start=False, stop=True, skip_group_check=True).then_inc(hist_done, 1)
            pe.matmul(b[1][0:HI, 0:LO], zerob[:, 0:HI], zerob[:, HI:HI + LO], start=False, stop=True, skip_group_check=True).then_inc(hist_done, 1)
            pe.wait_ge(const_in, 16)
            pe.wait_ge(kv_in, 16)
            for k in range(2):
                for s in range(8):
                    m = pe.transpose(b[2 + 2 * k + s // 4][:, (s % 4) * 128:(s % 4 + 1) * 128],
                                     wkvn[:, s, k * 128:(k + 1) * 128], g.ident)
                    if s % 4 == 3:
                        m.then_inc(wt_done, 1)
            pe.wait_ge(wo_in, 16)
            for q in range(4):
                for s in range(2):
                    m = pe.transpose(b[6 + q // 2][:, (q % 2) * 256 + s * 128:(q % 2) * 256 + (s + 1) * 128],
                                     won[:, s, q * 128:(q + 1) * 128], g.ident)
                if q % 2:
                    m.then_inc(wt_done, 1)

        @block.scalar
        def _(act):
            for k in range(2):
                for hf in range(2):
                    act.wait_ge(wt_done, 2 * k + hf + 1)
                    act.copy(g.wkvT[:, k, hf * 512:(hf + 1) * 512], b[2 + 2 * k + hf][:, :]).then_inc(wt_copied, 1)
            for q in range(2):
                act.wait_ge(wt_done, 5 + q)
                act.copy(g.woT[:, 2 * q:2 * q + 2, :], b[6 + q][:, :].rearrange("p (q c) -> p q c", q=2)).then_inc(wt_copied, 1)


def node_loop(nc, g):
    with ExitStack() as ctx:
        t = Parts(nc, ctx, "node")
        sb, sem, sems = t.sb, t.sem, t.sems
        S = EK // 2
        onehot = sb("onehot", [TP, 2, S, NB], BF16)
        junk = sb("junk", [TP, 2, NB])
        place = sb("place", [TP, EK])
        placei, slot = sb("placei", [TP, EK], I32), sb("slot", [TP, EK], I32)
        chunk = sb("chunk", [TP, EK], I32)
        where, load = sb("where", [TP, 2, EK], I32), sb("load", [TP, 2, EK], I32)
        xin = sb("xin", [TP, 2, D])
        stats, mv = sb("stats", [TP, 6]), sb("mv", [TP, 2])
        std, rstd = sb("std", [TP, 1]), sb("rstd", [TP, 1])
        kstd = sb("kstd", [TP, 2 * MH])
        xn = sb("xn", [TP, 2, D])
        xT = sb("xT", [128, 2, 2, TP])
        tab = sb("tab", [TP, 2, ROW])
        hlt = sb("hlt", [TP, 2, GH])
        kc, vc = sb("kc", [TP, 2, INNER]), sb("vc", [TP, 2, INNER])
        sq = sb("sq", [TP, 2, 2 * INNER])
        var, kvr, vs = sb("var", [TP, 2 * MH]), sb("kvr", [TP, 2 * MH]), sb("vs", [TP, 2, INNER])
        scl = sb("scl", [TP, MH])

        x_in = sems("x_in", 2)
        tab_out, hl_out = sems("tab_out", 2), sems("hl_out", 2)
        tones, onehot_ready, prefix_ready, prefix_read = sem("tones"), sem("onehot_ready"), sem("prefix_ready"), sem("prefix_read")
        counted = sem("counted")
        place_ready, slot_ready, where_ready = sem("place_ready"), sem("slot_ready"), sem("where_ready")
        scattered = sems("scattered", 2)
        stats_ready, mv_ready, std_ready, rstd_ready, xn_ready = (
            sem("stats_ready"), sem("mv_ready"), sem("std_ready"), sem("rstd_ready"), sem("xn_ready"))
        var_ready, kstd_ready = sem("var_ready"), sem("kstd_ready")
        xt_ready, xt_copied, xt_stored = sem("xt_ready"), sem("xt_copied"), sem("xt_stored")
        h_ready, tab_ready = sem("h_ready"), sem("tab_ready")
        kv_ready, kv_copied = sem("kv_ready"), sem("kv_copied")
        kv_step, vs_ready, dt_done = sem("kv_step"), sem("vs_ready"), sem("dt_done")
        block = ctx.enter_context(nc.Block())
        b = g.bank
        RB, XB, HB, KB, VB, DB = (b[0], b[1]), b[2], b[3], b[4], b[5], b[6]

        @block.sync
        def _(sp):
            def step(j, first):
                for k in range(2):
                    i = 2 * j + k
                    if not first:
                        sp.wait_ge(xn_ready, i - 1)
                    sp.dma_start(xin[:, k, :], g.x[ds(i * TP, TP), :]).then_inc(x_in[k], 16)
                for k in range(2):
                    i = 2 * j + k
                    sp.wait_ge(tab_ready, i + 1)
                    sp.dma_start(g.table_d[ds(i * TP, TP), :], tab[:, k, :]).then_inc(tab_out[k], 16)
                    sp.dma_start(g.hl_d[ds(i * TP, TP), :], hlt[:, k, :]).then_inc(hl_out[k], 16)
            step(0, True)
            with sp.Fori(1, NT // 2) as j:
                step(j, False)
            for k in range(2):
                sp.wait_ge(tab_out[k], 16 * (NT // 2))
                sp.wait_ge(hl_out[k], 16 * (NT // 2))

        @block.gpsimd
        def _(pool):
            with pool.Fori(0, NT // 2) as j:
                for k in range(2):
                    after(pool, g, where_ready, 2 * (2 * j + k) + 2)
                    for c in range(EK):
                        pool.indirect_dma_start(g.sorted_d, bass.IndirectOffsetOnAxis(ap=where[:, k, c:c + 1], axis=0),
                                                load[:, k, c:c + 1], None).then_inc(scattered[k], 16)
            for k in range(2):
                pool.wait_ge(scattered[k], 16 * EK * (NT // 2))

        @block.vector
        def _(v):
            v.memset(tab[:, :, :], 1.0).then_inc(tones, 1)

            def normalise(i, k):
                v.wait_ge(std_ready, i + 1)
                v.reciprocal(rstd[:, :], std[:, :]).then_inc(rstd_ready, 1)
                if not (isinstance(i, int) and i < 2):
                    v.wait_ge(xt_ready, i - 1)
                v.wait_ge(rstd_ready, i + 1)
                v.tensor_scalar(xn[:, k, :], xin[:, k, :], mv[:, 0:1], rstd[:, 0:1], ALU.subtract, ALU.mult).then_inc(xn_ready, 1)

            def variances(i, k):
                v.wait_ge(kv_copied, 4 * i + 4)
                v.tensor_reduce(var[:, :], sq[:, k, :].rearrange("p (h f) -> p h f", f=MF), axis=AX.X, op=ALU.add).then_inc(var_ready, 1)

            def scale_values(i, k):
                v.wait_ge(kstd_ready, i + 1)
                v.reciprocal(kvr[:, :], kstd[:, :]).then_inc(kv_step, 1)
                v.wait_ge(kv_step, 2 * i + 1)
                v.tensor_tensor(scl[:, :], kvr[:, 0:MH], kvr[:, MH:2 * MH], ALU.mult).then_inc(kv_step, 1)
                v.wait_ge(kv_step, 2 * i + 2)
                v.tensor_tensor(vs[:, k, :].rearrange("p (h f) -> p h f", f=MF),
                                vc[:, k, :].rearrange("p (h f) -> p h f", f=MF),
                                bc(scl[:, :].unsqueeze(2), [TP, MH, MF]), ALU.mult).then_inc(vs_ready, 1)

            def step(j, first):
                for k in range(2):
                    i = 2 * j + k
                    if not (first and k == 0):
                        v.wait_ge(counted, 2 * i)
                    v.wait_ge(x_in[k], 16 * j + 16)
                    v.bn_stats(stats[:, :], xin[:, k, :]).then_inc(stats_ready, 1)
                    for s in range(2):
                        for c in range(S):
                            if s * S + c == EK - 1:
                                v.wait_ge(stats_ready, i + 1)
                            v.tensor_scalar(onehot[:, s, c, :], g.iotab[0:TP, :], g.bktf[:, ds(i * S + (s * HALF + c), 1)],
                                            None, ALU.is_equal).then_inc(onehot_ready, 1)
                    v.bn_aggr(mv[:, :], stats[:, :]).then_inc(mv_ready, 1)
                    if not (first and k == 0):
                        variances(i - 1, 1 - k)
                    for c in range(S):
                        if c == 4:
                            normalise(i, k)
                        if c == 6 and not (first and k == 0):
                            scale_values(i - 1, 1 - k)
                        for s in range(2):
                            n = c * 2 + s
                            v.wait_ge(prefix_ready, EK * i + (n + 1))
                            if not (first and k == 0 and n < 2):
                                v.wait_ge(prefix_read, EK * i + (n - 1))
                            v.scalar_tensor_tensor(junk[:, s, :], onehot[:, s, c, :], 1.0, RB[s][0:TP, 0:NB], ALU.mult, ALU.mult,
                                                   accum_out=place[:, n:n + 1]).then_inc(prefix_read, 1)
                    v.wait_ge(prefix_read, EK * i + EK)
                    v.tensor_copy(placei[:, :], place[:, :]).then_inc(place_ready, 1)
                    v.wait_ge(place_ready, i + 1)
                    v.tensor_scalar(slot[:, :], placei[:, :], 127, None, ALU.bitwise_and).then_inc(slot_ready, 1)
                    v.tensor_scalar(chunk[:, :], placei[:, :], 7, None, ALU.arith_shift_right).then_inc(slot_ready, 1)
                    v.wait_ge(slot_ready, 2 * i + 2)
                    if not first:
                        v.wait_ge(scattered[k], 16 * EK * j)
                    v.scalar_tensor_tensor(where[:, k, :], slot[:, :], float(NCH), chunk[:, :], ALU.mult, ALU.add).then_inc(where_ready, 1)
                    v.tensor_copy(load[:, k, :].rearrange("p (c s) -> p s c", s=2),
                                  g.packi[:, :].rearrange("p (s c) -> p s c", s=2)[:, :, ds(i * S, S)]).then_inc(where_ready, 1)
            step(0, True)
            with v.Fori(1, NT // 2) as j:
                step(j, False)
            variances(NT - 1, 1)
            scale_values(NT - 1, 1)

        @block.tensor
        def _(pe):
            for s in range(2):
                pe.matmul(RB[s][:, 0:NB], g.ones[0:1, :], g.firsts[0:1, s, :], start=True, stop=True)
            pe.matmul(DB[:, :], g.zero[:, 0:128], g.zero[:, :], start=True, stop=True)

            def product(i, k):
                pe.wait_ge(vs_ready, i + 1)
                for p in range(4):
                    m = pe.matmul(DB[:, p * 128:(p + 1) * 128], vs[:, k, p * 128:(p + 1) * 128], kc[:, k, p * 128:(p + 1) * 128],
                                  start=False, stop=True, skip_group_check=True)
                m.then_inc(dt_done, 1)

            def step(j, first):
                for k in range(2):
                    i = 2 * j + k
                    for c in range(S + 1):
                        for s in range(2):
                            if c > 0:
                                pe.wait_ge(prefix_read, EK * i + (2 * c + s - 1))
                                m = pe.matmul(RB[s][0:TP, 0:NB], g.geb[0:TP, 0:TP], onehot[:, s, c - 1, :], start=False, stop=True, skip_group_check=True)
                                if c == S:
                                    m.then_inc(counted, 1)
                            if c < S:
                                pe.wait_ge(onehot_ready, EK * i + (s * S + c + 1))
                                pe.matmul(RB[s][0:TP, 0:NB], g.ltb[0:TP, 0:TP], onehot[:, s, c, :], start=False, stop=True, skip_group_check=True).then_inc(prefix_ready, 1)
                    pe.wait_ge(xn_ready, i + 1)
                    if not (first and k == 0):
                        pe.wait_ge(xt_copied, 2 * i)
                    for q in range(2):
                        m = pe.transpose(XB[:, q * 128:q * 128 + TP], xn[:, k, q * 128:(q + 1) * 128], g.ident[0:TP, 0:TP])
                    m.then_inc(xt_ready, 1)
                    pe.wait_ge(xt_copied, 2 * i + 1)
                    if not (first and k == 0):
                        pe.wait_ge(tab_ready, i)
                    for q in range(2):
                        m = pe.matmul(HB[0:TP, 0:D + 2 * GH], xT[:, k, q, :], g.wa[:, q, :], start=(q == 0), stop=(q == 1))
                    m.then_inc(h_ready, 1)
                    if not (first and k == 0):
                        pe.wait_ge(kv_copied, 4 * i)
                    for w, bk in ((0, KB), (1, VB)):
                        for q in range(2):
                            m = pe.matmul(bk[0:TP, :], xT[:, k, q, :], g.wkvT[:, q, w * INNER:(w + 1) * INNER], start=(q == 0), stop=(q == 1))
                        m.then_inc(kv_ready, 1)
                    if not (first and k == 0):
                        product(i - 1, 1 - k)
            step(0, True)
            with pe.Fori(1, NT // 2) as j:
                step(j, False)
            product(NT - 1, 1)

        @block.scalar
        def _(act):
            def heads(i):
                act.wait_ge(var_ready, i + 1)
                act.activation(kstd[:, :], var[:, :], ACT.Sqrt, bias=g.eps[0:TP, :], scale=1.0 / MF).then_inc(kstd_ready, 1)

            def step(j, first):
                for k in range(2):
                    i = 2 * j + k
                    act.wait_ge(mv_ready, i + 1)
                    act.activation(std[:, :], mv[:, 1:2], ACT.Sqrt, bias=g.eps[0:TP, :]).then_inc(std_ready, 1)
                    if not (first and k == 0):
                        heads(i - 1)
                    act.wait_ge(xt_ready, i + 1)
                    if not first:
                        act.wait_ge(kv_ready, 2 * i - 2)
                    xb = XB[:, 0:256].rearrange("p (q n) -> p q n", q=2)[:, :, 0:TP]
                    act.copy(xT[:, k, :, :], xb).then_inc(xt_copied, 1)
                    act.copy(g.xnT[:, ds(i, 1), :, :].rearrange("p a q n -> p (a q) n"), xb).then_inc(xt_copied, 1)
                    act.wait_ge(h_ready, i + 1)
                    if first and k == 0:
                        act.wait_ge(tones, 1)
                    if not first:
                        act.wait_ge(tab_out[k], 16 * j)
                        act.wait_ge(hl_out[k], 16 * j)
                    act.copy(tab[:, k, 0:TW].rearrange("p (h f) -> p h f", f=HW)[:, :, 0:GF],
                             HB[0:TP, 0:D].rearrange("p (h f) -> p h f", f=GF))
                    act.copy(tab[:, k, TW:ROW], HB[0:TP, D:D + GH])
                    act.copy(hlt[:, k, :], HB[0:TP, D + GH:D + 2 * GH]).then_inc(tab_ready, 1)
                    if not first:
                        act.wait_ge(dt_done, i - 1)
                        act.wait_ge(vs_ready, i - 1)
                    for w, (bk, kept) in enumerate(((KB, kc), (VB, vc))):
                        act.wait_ge(kv_ready, 2 * i + (w + 1))
                        act.copy(kept[:, k, :], bk[0:TP, :]).then_inc(kv_copied, 1)
                        act.activation(sq[:, k, w * INNER:(w + 1) * INNER], bk[0:TP, :], ACT.Square).then_inc(kv_copied, 1)
            step(0, True)
            with act.Fori(1, NT // 2) as j:
                step(j, False)
            heads(NT - 1)


def chunk_tables(nc, g):
    with ExitStack() as ctx:
        t = Parts(nc, ctx, "chunks")
        sb, sem = t.sb, t.sem
        packed = sb("packed", [128, NCH], I32)
        loci = sb("loci", [128, NCH], I32)
        fc, ec = sb("fc", [NBT, 2]), sb("ec", [NBT, 2])
        below, oh, starts = sb("below", [NBT, 2, NCH]), sb("oh", [NBT, 2, NCH]), sb("starts", [NBT, 2, NCH])
        hlb = sb("hlb", [NBT, 2, BR * GH])
        hlp = sb("hlp", [NBT, 2, GH, BR])
        base, nf, ni = sb("base", [NBT, 2]), sb("nf", [NBT, 2, BR]), sb("ni", [NBT, 2, BR], I32)
        dT, mixA = sb("dT", [128, 4, 128]), sb("mixA", [128, 4, D])
        list_in, cols_in, hl_in, n_out, n_in = sem("list_in"), sem("cols_in"), sem("hl_in"), sem("n_out"), sem("n_in")
        unpack, table, hlp_ready, oh_ready, st_ready = sem("unpack"), sem("table"), sem("hlp_ready"), sem("oh_ready"), sem("st_ready")
        n_step, n_ready, dz, dt_ready = sem("n_step"), sem("n_ready"), sem("dz"), sem("dt_ready")
        a_done, a_ready, p_done = sem("a_done"), sem("a_ready"), sem("p_done")
        rows_done = sem("rows_done")
        block = ctx.enter_context(nc.Block())
        b = g.bank
        H = NCH // 2

        @block.sync
        def _(sp):
            sp.dma_start(packed[:, :], g.sorted_d.rearrange("(p c) a -> p (c a)", p=128)).then_inc(list_in, 16)
            for s, dst in ((0, fc), (1, ec)):
                sp.dma_start(dst[:, :], g.cols_d[s, :].rearrange("(p t) -> p t", t=2)).then_inc(cols_in, 16)
            sp.dma_start(hlb[:, :, :], g.hl_d.rearrange("(p t r) h -> p t (r h)", t=2, r=BR)).then_inc(hl_in, 16)
            sp.wait_ge(n_ready, 1)
            sp.dma_start(g.node_d.rearrange("(p t r) a -> p t (r a)", t=2, r=BR), ni[:, :, :]).then_inc(n_out, 16)
            sp.wait_ge(n_out, 16)
            sp.dma_start(g.nodeidx[:, :], g.node_d[0:N, :].rearrange("(t p) a -> p (t a)", p=TP),
                         allow_slow_non_contiguous=True).then_inc(n_in, 16)
            sp.wait_ge(n_in, 16)

        @block.vector
        def _(v):
            v.wait_ge(list_in, 16)
            v.tensor_scalar(g.colidx[:, :], packed[:, :], (1 << COLBITS) - 1, None, ALU.bitwise_and)
            v.tensor_scalar(loci[:, :], packed[:, :], COLBITS, None, ALU.arith_shift_right).then_inc(unpack, 1)
            v.wait_ge(unpack, 1)
            v.tensor_copy(g.local[:, :], loci[:, :])
            v.wait_ge(hl_in, 16)
            v.tensor_copy(hlp[:, :, :, :], hlb[:, :, :].rearrange("p t (r h) -> p t h r", h=GH)).then_inc(hlp_ready, 1)
            v.wait_ge(cols_in, 32)
            io = g.iota[0:NBT, :]
            for s in range(2):
                v.tensor_scalar(below[:, s, :], io, ec[:, s:s + 1], None, ALU.is_lt).then_inc(table, 1)
                v.wait_ge(table, s + 1)
                v.scalar_tensor_tensor(oh[:, s, :], io, fc[:, s:s + 1], below[:, s, :], ALU.is_ge, ALU.mult).then_inc(oh_ready, 1)
                v.tensor_scalar(starts[:, s, :], io, fc[:, s:s + 1], -BIG, ALU.is_equal, ALU.mult).then_inc(st_ready, 1)
            v.tensor_scalar(base[:, :], ec[:, :], -1.0, float(BR), ALU.add, ALU.mult).then_inc(n_step, 1)
            v.wait_ge(n_step, 1)
            for s in range(2):
                v.tensor_scalar(nf[:, s, :], io[:, 0:BR], base[:, s:s + 1], None, ALU.add).then_inc(n_step, 1)
            v.wait_ge(n_step, 3)
            v.tensor_copy(ni[:, :, :], nf[:, :, :]).then_inc(n_ready, 1)
            v.memset(dT[:, :, :], 0.0).then_inc(dz, 1)
            v.wait_ge(dz, 1)
            for h in range(2):
                r = slice(64 * h, 64 * h + 64)
                v.tensor_copy(dT[r, :, r], b[6][r, :].rearrange("p (q c) -> p q c", q=4)[:, :, r]).then_inc(dt_ready, 1)
            v.wait_ge(rows_done, 4)
            for hf in range(2):
                v.tensor_copy(g.hlc[:, hf * H:(hf + 1) * H], b[hf][:, 0:H])
                v.tensor_copy(g.reset[:, hf * H:(hf + 1) * H], b[2 + hf][:, 0:H])
            for q in range(2):
                v.wait_ge(a_done, q + 1)
                v.tensor_copy(mixA[:, 2 * q:2 * q + 2, :], b[4 + q][:, :].rearrange("p (q c) -> p q c", q=2)).then_inc(a_ready, 1)
            v.wait_ge(p_done, 1)
            v.tensor_scalar(g.mixP[:, :, :], b[7][:, :].rearrange("p (q c) -> p q c", q=2), 1.0 / N, None, ALU.mult)

        @block.tensor
        def _(pe):
            pe.wait_ge(hlp_ready, 1)
            pe.wait_ge(oh_ready, 2)
            for hf in range(2):
                for s in range(2):
                    m = pe.matmul(b[hf][:, 0:H], hlp[:, s, :, :], oh[:, s, hf * H:(hf + 1) * H], start=(s == 0), stop=(s == 1))
                m.then_inc(rows_done, 1)
            pe.wait_ge(st_ready, 2)
            for hf in range(2):
                for s in range(2):
                    m = pe.matmul(b[2 + hf][:, 0:H], g.ones[0:NBT, :], starts[:, s, hf * H:(hf + 1) * H], start=(s == 0), stop=(s == 1))
                m.then_inc(rows_done, 1)
            pe.wait_ge(dt_ready, 2)
            for q in range(4):
                m = pe.matmul(b[4 + q // 2][:, (q % 2) * D:(q % 2 + 1) * D], dT[:, q, :], g.woT[:, q, :], start=True, stop=True)
                if q % 2:
                    m.then_inc(a_done, 1)
            pe.wait_ge(a_ready, 2)
            for k in range(2):
                for q in range(4):
                    m = pe.matmul(b[7][:, k * D:(k + 1) * D], g.wq[:, q, k * 128:(k + 1) * 128], mixA[:, q, :],
                                  start=(q == 0), stop=(q == 3))
            m.then_inc(p_done, 1)


def edge_loop(nc, g):
    with ExitStack() as ctx:
        t = Parts(nc, ctx, "edge")
        sb, sem, sems = t.sb, t.sem, t.sems
        gat = sb("gat", [128, RING, GU, ROW])
        idx = sb("idx", [128, 2, RING * GU // 2], I32)
        mask = sb("mask", [128, 2, GU, BR])
        scr = sb("scr", [128, 2, GU, GH, BR])
        mch = sb("mch", [128, 2, GU])
        mrun, srun = sb("mrun", [128, 2, GU]), sb("srun", [128, 2, 1 + GU])
        zrun = sb("zrun", [128, GU])
        bias1, bias2 = sb("bias1", [128, 2, GU]), sb("bias2", [128, 2, GU])
        dif, dif2, fac = sb("dif", [128, GU]), sb("dif2", [128, 3, GU]), sb("fac", [128, 3, GU])
        hl2 = sb("hl2", [128, NCH])
        e1, e2 = sb("e1", [128, 2, GU * 128]), sb("e2", [128, 2, GU * 128])
        wt = sb("wt", [128, 2, GU * 128])
        wts = sb("wts", [128, 2, GU * 128])
        acc = sb("acc", [128, 3, GU, HW])

        gathered = sems("gathered", RING)
        idx_ready = sem("idx_ready")
        init = sem("init")
        mask_ready, scr_ready, scr_used = sem("mask_ready"), sem("scr_ready"), sem("scr_used")
        mch_ready, mrun_ready, zrun_ready, srun_ready = sem("mch_ready"), sem("mrun_ready"), sem("zrun_ready"), sem("srun_ready")
        bias_ready, dif_ready, dif2_ready = sem("bias_ready"), sem("dif_ready"), sem("dif2_ready")
        exp_ready, fac_ready, wt_ready, wtt_ready, wts_ready = sem("exp_ready"), sem("fac_ready"), sem("wt_ready"), sem("wtt_ready"), sem("wts_ready")
        agg_ready, acc_ready = sem("agg_ready"), sem("acc_ready")
        sums_out = sems("sums_out", 3)
        block = ctx.enter_context(nc.Block())
        ST, WB, AB = g.bank[0:2], g.bank[2:4], g.bank[4:6]

        def groups(eng, step):
            for u in range(RING):
                step(u, u, 0, False)
            with eng.Fori(1, NG // RING) as m:
                for u in range(RING):
                    step(m * RING + u, u, m, True)

        @block.gpsimd
        def _(pool):
            hf = RING * GU // 2

            def indices(half, c0, n, first):
                if not first:
                    for u in range(3 * half, 3 * half + 3):
                        pool.wait_ge(gathered[u], 16 * GU * n)
                pool.tensor_copy(idx[:, half, :], g.colidx[:, ds(c0, hf)]).then_inc(idx_ready, 1)

            def body(m, first):
                for half in range(2):
                    indices(half, m * (2 * hf) + half * hf, m, first)
                    after(pool, g, idx_ready, 2 * m + (half + 1))
                    for u in range(3 * half, 3 * half + 3):
                        if not first:
                            after(pool, g, agg_ready, m * RING + (u - RING + 1))
                        for c in range(GU):
                            pool.indirect_dma_start(gat[:, u, c, :], None, g.table_d,
                                                    bass.IndirectOffsetOnAxis(ap=idx[:, half, (u % 3) * GU + c:(u % 3) * GU + c + 1], axis=0)
                                                    ).then_inc(gathered[u], 16)
            body(0, True)
            with pool.Fori(1, NG // RING) as m:
                body(m, False)

        @block.vector
        def _(v):
            v.tensor_scalar(hl2[:, :], g.hlc[:, :], SLOPE, None, ALU.mult)
            v.memset(mrun[:, 1, :], -BIG)
            v.memset(srun[:, 1, :], -BIG)
            v.memset(acc[:, 2, :, :], 0.0).then_inc(init, 1)
            v.wait_ge(init, 1)

            def A1(n, u, m, late):
                k = u % 2
                if late or u >= 2:
                    v.wait_ge(scr_ready, 2 * (n - 1))
                for c in range(GU):
                    i = v.tensor_scalar(mask[:, k, c, :], g.iota[:, 0:BR], g.local[:, ds(n * GU + c, 1)], -BIG,
                                        ALU.not_equal, ALU.mult)
                i.then_inc(mask_ready, 1)

            def A2(n, u, m, late):
                k = u % 2
                v.wait_ge(gathered[u], 16 * GU * (m + 1))
                v.wait_ge(mask_ready, n + 1)
                if late or u >= 2:
                    v.wait_ge(scr_used, n - 1)
                for c in range(GU):
                    i = v.tensor_tensor(scr[:, k, c, :, :], bc(mask[:, k, c, :].unsqueeze(1), [128, GH, BR]),
                                        bc(gat[:, u, c, TW:ROW].unsqueeze(2), [128, GH, BR]), ALU.add)
                    if c % 2:
                        i.then_inc(scr_ready, 1)

            def chain(n, u, k):
                o, t3 = 1 - k, u % 3
                hl = g.hlc[:, ds(n * GU, GU)]
                cols = ds(n * GU, GU)

                def b1():
                    v.wait_ge(scr_used, n + 1)
                    v.tensor_reduce(mch[:, k, :], ST[k][:, :].rearrange("p (c e) -> p c e", c=GU), axis=AX.X, op=ALU.max).then_inc(mch_ready, 1)

                def b2():
                    v.wait_ge(mch_ready, n + 1)
                    v.tensor_tensor_scan(mrun[:, k, :], g.reset[:, cols], mch[:, k, :], mrun[:, o, GU - 1:GU], ALU.add, ALU.max).then_inc(mrun_ready, 1)

                def b3():
                    v.wait_ge(mrun_ready, n + 1)
                    v.scalar_tensor_tensor(zrun[:, :], mrun[:, k, :], -FLOOR, hl, ALU.max, ALU.add).then_inc(zrun_ready, 1)

                def b4():
                    v.wait_ge(zrun_ready, n + 1)
                    v.scalar_tensor_tensor(srun[:, k, 1:1 + GU], zrun[:, :], SLOPE, zrun[:, :], ALU.mult, ALU.max).then_inc(srun_ready, 1)

                def b5():
                    v.wait_ge(srun_ready, n + 1)
                    v.tensor_tensor(bias1[:, k, :], hl, srun[:, k, 1:1 + GU], ALU.subtract)
                    v.tensor_tensor(bias2[:, k, :], hl2[:, cols], srun[:, k, 1:1 + GU], ALU.subtract).then_inc(bias_ready, 1)
                    v.tensor_tensor(dif[:, 1:GU], srun[:, k, 1:GU], srun[:, k, 2:1 + GU], ALU.subtract)
                    v.tensor_tensor(dif[:, 0:1], srun[:, o, GU:1 + GU], srun[:, k, 1:2], ALU.subtract).then_inc(dif_ready, 1)

                def b6():
                    v.wait_ge(dif_ready, n + 1)
                    v.tensor_tensor(dif2[:, t3, :], dif[:, :], g.reset[:, cols], ALU.add).then_inc(dif2_ready, 1)
                return [b1, b2, b3, b4, b5, b6]

            def C1(n, k):
                v.wait_ge(exp_ready, n + 1)
                v.tensor_tensor(wt[:, k, :], e1[:, k, :], e2[:, k, :], ALU.max).then_inc(wt_ready, 1)

            def sums(n, u):
                k, r, o = u % 2, u % 3, (u - 1) % 3

                def d(c):
                    def f():
                        if c == 0:
                            v.wait_ge(agg_ready, n + 1)
                            v.wait_ge(fac_ready, n + 1)
                        before = acc[:, r, c - 1, :] if c else acc[:, o, GU - 1, :]
                        if not (isinstance(n, int) and n == 0 and c == 0):
                            v.wait_ge(acc_ready, n * GU + c)
                        if c == 0 and not (isinstance(n, int) and n < 3):
                            v.wait_ge(sums_out[r], 64 * free(n, r))
                        v.scalar_tensor_tensor(acc[:, r, c, :], before, fac[:, r, c:c + 1], AB[k][:, c * HW:(c + 1) * HW],
                                               ALU.mult, ALU.add).then_inc(acc_ready, 1)
                    return f
                return [d(c) for c in range(GU)]

            uses = {}

            def free(n, r):
                return uses[r]

            def step(n, u, m, late):
                real = (lambda q: late or n >= q)
                b = chain(n - 1, (u - 1) % RING, (u - 1) % 2) if real(1) else [lambda: None] * 6
                if real(4):
                    uses[(u - 4) % 3] = 2 * m + (u - 4) // 3
                    d = sums(n - 4, (u - 4) % RING)
                else:
                    d = [lambda: None] * GU
                b[0]()
                d[0]()
                b[1]()
                d[1]()
                b[2]()
                d[2]()
                b[3]()
                A1(n, u, m, late)
                b[4]()
                b[5]()
                A2(n, u, m, late)
                d[3]()
                if real(2):
                    C1(n - 2, u % 2)
            groups(v, step)
            for n in range(NG, NG + 4):
                u = n % RING
                uses[(u - 4) % 3] = (n - 4) // 3
                if n == NG:
                    for f in chain(n - 1, (u - 1) % RING, (u - 1) % 2):
                        f()
                for f in sums(n - 4, (u - 4) % RING):
                    f()
                if n <= NG + 1:
                    C1(n - 2, u % 2)

        @block.tensor
        def _(pe):
            def scores(n, u):
                k = u % 2
                if not (isinstance(n, int) and n < 2):
                    pe.wait_ge(exp_ready, n - 1)
                for c in range(GU):
                    if c % 2 == 0:
                        pe.wait_ge(scr_ready, 2 * n + c // 2 + 1)
                    m = pe.transpose(ST[k][:, c * 128:(c + 1) * 128], scr[:, k, c, :, :].rearrange("p h r -> p (h r)"), g.ident)
                m.then_inc(scr_used, 1)

            def weights(n, u):
                k = u % 2
                pe.wait_ge(wt_ready, n + 1)
                if not (isinstance(n, int) and n < 2):
                    pe.wait_ge(wts_ready, n - 1)
                for c in range(GU):
                    m = pe.transpose(WB[k][:, c * 128:(c + 1) * 128], wt[:, k, c * 128:(c + 1) * 128], g.ident)
                m.then_inc(wtt_ready, 1)

            def aggregate(n, u):
                k = u % 2
                pe.wait_ge(wts_ready, n + 1)
                if not (isinstance(n, int) and n < 2):
                    pe.wait_ge(acc_ready, GU * (n - 1))
                for c in range(GU):
                    for h in range(GH):
                        m = pe.matmul(AB[k][h * BR:(h + 1) * BR, c * HW:(c + 1) * HW],
                                      wts[:, k, c * 128 + h * BR:c * 128 + (h + 1) * BR], gat[:, u, c, h * HW:(h + 1) * HW],
                                      start=True, stop=True)
                m.then_inc(agg_ready, 1)

            def step(n, u, m, late):
                scores(n, u)
                if late or n >= 2:
                    weights(n - 2, (u - 2) % RING)
                    aggregate(n - 2, (u - 2) % RING)
            groups(pe, step)
            for n in range(NG - 2, NG):
                weights(n, n % RING)
                aggregate(n, n % RING)

        @block.scalar
        def _(act):
            def exps(n, u):
                k = u % 2
                act.wait_ge(bias_ready, n + 1)
                if not (isinstance(n, int) and n < 2):
                    act.wait_ge(wt_ready, n - 1)
                for c in range(GU):
                    s = slice(c * 128, (c + 1) * 128)
                    act.activation(e1[:, k, s], ST[k][:, s], ACT.Exp, bias=bias1[:, k, c:c + 1])
                    i = act.activation(e2[:, k, s], ST[k][:, s], ACT.Exp, bias=bias2[:, k, c:c + 1], scale=SLOPE)
                i.then_inc(exp_ready, 1)
                act.wait_ge(dif2_ready, n + 1)
                if not (isinstance(n, int) and n < 3):
                    act.wait_ge(acc_ready, GU * (n - 2))
                act.activation(fac[:, u % 3, :], dif2[:, u % 3, :], ACT.Exp).then_inc(fac_ready, 1)

            def copy(n, u):
                k = u % 2
                act.wait_ge(wtt_ready, n + 1)
                if not (isinstance(n, int) and n < 2):
                    act.wait_ge(agg_ready, n - 1)
                act.copy(wts[:, k, :], WB[k][:, :]).then_inc(wts_ready, 1)

            def step(n, u, m, late):
                if late or n >= 1:
                    exps(n - 1, (u - 1) % RING)
                if late or n >= 2:
                    copy(n - 2, (u - 2) % RING)
            groups(act, step)
            exps(NG - 1, (NG - 1) % RING)
            copy(NG - 2, (NG - 2) % RING)
            copy(NG - 1, (NG - 1) % RING)

        @block.sync
        def _(sp):
            out = g.sums_d.rearrange("(c r) (h f) -> h r c f", r=BR, h=GH)

            def step(n, u, m, late):
                sp.wait_ge(acc_ready, GU * (n + 1))
                for h in range(GH):
                    sp.dma_start(out[h][:, ds(n * GU, GU), :], acc[h * BR:(h + 1) * BR, u % 3, :, :]).then_inc(sums_out[u % 3], 16)
            groups(sp, step)
            for r in range(3):
                sp.wait_ge(sums_out[r], 64 * (NG // 3))


def token_loop(nc, g):
    with ExitStack() as ctx:
        t = Parts(nc, ctx, "token")
        sb, sem, sems = t.sb, t.sem, t.sems
        idx = sb("tidx", [TP, 2, TB], I32)
        sums = sb("sums", [TP, 2, TB, TW])
        xin = sb("txin", [TP, 2, TB, D])
        x2 = sb("x2", [TP, 2, TB, D])
        xf = sb("xf", [TP, 2, TB, D])
        xTs = sb("xTs", [128, 2, 2, TP])
        den, rden = sb("den", [TP, TB, GH]), sb("rden", [TP, TB, GH])
        stats, mv = sb("tstats", [TP, TB, 6]), sb("tmv", [TP, TB, 2])
        var2, std2, r12 = sb("var2", [TP, TB]), sb("std2", [TP, TB]), sb("r12", [TP, TB])
        gbc, bbc = sb("gbc", [TP, D]), sb("bbc", [TP, D])
        xfT = sb("xfT", [128, 2, 2, TP])
        lg = sb("lg", [TP, TB, NE])
        top, topi, topf = sb("top", [TP, TB, NE]), sb("topi", [TP, TB, NE], U32), sb("topf", [TP, TB, NE])
        one1, one2 = sb("one1", [TP, TB, NE]), sb("one2", [TP, TB, NE])
        both = sb("both", [TP, TB, NE], BF16)
        base, ranks = sb("base", [TP, NE]), sb("ranks", [TP, TB, NE])
        pj = sb("pj", [TP, 2, TB, NE])
        pos = sb("pos", [TP, 2, TB])
        posi = sb("posi", [TP, 2, 2, TB], I32)
        dl, el, el1 = sb("dl", [TP, TB]), sb("el", [TP, TB]), sb("el1", [TP, TB])
        onesb = sb("onesb", [TP, 128], BF16)
        ebase = sb("ebase", [128, NE])
        cnts, cnti, cntj, nch = sb("cnts", [128, NE]), sb("cnti", [128, NE], I32), sb("cntj", [128, NE], I32), sb("nch", [128, NE])
        ends, begin, last = sb("ends", [128, NE]), sb("begin", [128, NE]), sb("last", [128, 1])
        prow, pcol = sb("prow", [128, 1]), sb("pcol", [128, 1])
        padi = sb("padi", [128, NE], I32)
        zrow = sb("zrow", [128, D])
        chc, past, pastn = sb("chc", [1, MC]), sb("past", [1, NE - 1, MC]), sb("pastn", [1, NE - 1, MC])
        ex, bg, df, rw = sb("ex", [1, MC]), sb("bg", [1, MC]), sb("df", [1, MC]), sb("rw", [1, MC])
        delta = sb("delta", [128, NE])
        yd, yacc = sb("yd", [TP, NE, 2 * NT]), sb("yacc", [TP, NE, 2 * NT])

        gb_in = sem("gb_in")
        x_in, sums_in = sems("tx_in", 2), sems("sums_in", 2)
        x2_out, sent = sems("x2_out", 2), sems("sent", 2)
        idx_ready = sem("tidx_ready")
        xts_ready, mix_ready, mix_read = sem("xts_ready"), sem("mix_ready"), sem("mix_read")
        front_step, back_step, end_step = sem("front_step"), sem("back_step"), sem("end_step")
        sums_used, x2_ready, xf_ready, pos_ready = sem("sums_used"), sem("x2_ready"), sem("xf_ready"), sem("pos_ready")
        xft_ready, xft_copied, lg_ready, lg_read = sem("xft_ready"), sem("xft_copied"), sem("lg_ready"), sem("lg_read")
        var2_ready, std2_ready = sem("var2_ready"), sem("std2_ready")
        diff_ready, el_ready = sem("diff_ready"), sem("el_ready")
        both_ready, rank_ready, rank_read, total_ready = sem("both_ready"), sem("rank_ready"), sem("rank_read"), sem("total_ready")
        base_read, ebase_ready, pad_ready, pad_out = sem("base_read"), sem("ebase_ready"), sem("pad_ready"), sem("pad_out")
        block = ctx.enter_context(nc.Block())
        b = g.bank
        MB, XB, LB, PB, RB = b[0:2], b[2:4], b[4], b[5], b[6]

        def view(ap, m):
            return ap[ds(m * (TB * TP), TB * TP), :].rearrange("(t p) f -> p t f", p=TP)

        @block.sync
        def _(sp):
            sp.dma_start(gbc[:, :], g.gamma.partition_broadcast(TP)).then_inc(gb_in, 16)
            sp.dma_start(bbc[:, :], g.beta.partition_broadcast(TP)).then_inc(gb_in, 16)

            def step(j, first):
                for k in range(2):
                    m = 2 * j + k
                    if not first:
                        sp.wait_ge(sums_used, 2 * m - 2)
                    sp.dma_start(xin[:, k, :, :], view(g.x, m)).then_inc(x_in[k], 16)
                for k in range(2):
                    m = 2 * j + k
                    sp.wait_ge(x2_ready, m + 1)
                    sp.dma_start(view(g.x2_d, m), x2[:, k, :, :]).then_inc(x2_out[k], 16)
            step(0, True)
            with sp.Fori(1, NBL // 2) as j:
                step(j, False)
            for k in range(2):
                sp.wait_ge(x2_out[k], 16 * (NBL // 2))

        @block.gpsimd
        def _(pool):
            pool.memset(zrow[:, :], 0.0).then_inc(pad_ready, 1)

            def fetch(m, j, k, first):
                if not first:
                    pool.wait_ge(sums_in[k], 16 * TB * j)
                pool.tensor_copy(idx[:, k, :], g.nodeidx[:, ds(m * TB, TB)]).then_inc(idx_ready, 1)
                if not first:
                    pool.wait_ge(sums_used, 2 * m - 2)
                after(pool, g, idx_ready, m + 1)
                for c in range(TB):
                    pool.indirect_dma_start(sums[:, k, c, :], None, g.sums_d,
                                            bass.IndirectOffsetOnAxis(ap=idx[:, k, c:c + 1], axis=0)).then_inc(sums_in[k], 16)

            def send(m, k):
                after(pool, g, pos_ready, m + 1)
                for s in range(2):
                    for c in range(TB):
                        pool.indirect_dma_start(g.xs_d, bass.IndirectOffsetOnAxis(ap=posi[:, k, s, c:c + 1], axis=0),
                                                xf[:, k, c, :], None).then_inc(sent[k], 16)

            fetch(0, 0, 0, True)
            fetch(1, 0, 1, True)
            send(0, 0)
            with pool.Fori(1, NBL // 2) as j:
                for k in range(2):
                    fetch(2 * j + k, j, k, False)
                    send(2 * j + (k - 1), 1 - k)
            send(NBL - 1, 1)
            pool.wait_ge(pad_ready, 2)
            for e in range(NE):
                pool.indirect_dma_start(g.xs_d, bass.IndirectOffsetOnAxis(ap=padi[:, e:e + 1], axis=0), zrow[:, :], None).then_inc(pad_out, 16)
            for k in range(2):
                pool.wait_ge(sent[k], 32 * TB * (NBL // 2))
            pool.wait_ge(pad_out, 16 * NE)

        @block.scalar
        def _(act):
            def front(m, k, first):
                for c in range(TB):
                    i = m * TB + c
                    r = (k * TB + c) % 2
                    if not (first and k * TB + c < 2):
                        act.wait_ge(mix_ready, i - 1)
                    act.copy(xTs[:, r, :, :], g.xnT[:, ds(i, 1), :, :].rearrange("p a q n -> p (a q) n")).then_inc(xts_ready, 1)
                act.wait_ge(var2_ready, m + 1)
                act.activation(std2[:, :], var2[:, :], ACT.Sqrt).then_inc(std2_ready, 1)

            def back(m, k, first):
                for c in range(TB):
                    i = m * TB + c
                    r = (k * TB + c) % 2
                    act.wait_ge(xft_ready, i + 1)
                    act.copy(xfT[:, r, :, :], XB[r][:, 0:256].rearrange("p (q n) -> p q n", q=2)[:, :, 0:TP]).then_inc(xft_copied, 1)
                act.wait_ge(diff_ready, m + 1)
                act.activation(el[:, :], dl[:, :], ACT.Exp).then_inc(el_ready, 1)
            front(0, 0, True)
            front(1, 1, True)
            back(0, 0, True)
            with act.Fori(1, NBL // 2) as j:
                for k in range(2):
                    front(2 * j + k, k, False)
                    back(2 * j + (k - 1), 1 - k, False)
            back(NBL - 1, 1, False)

        @block.tensor
        def _(pe):
            pe.wait_ge(ebase_ready, 1)
            pe.matmul(RB[:, 0:NE], g.ones[0:1, :], ebase[0:1, :], start=True, stop=True).then_inc(total_ready, 1)

            def front(m, k, first):
                for c in range(TB):
                    i = m * TB + c
                    r = (k * TB + c) % 2
                    pe.wait_ge(xts_ready, i + 1)
                    if not (first and k * TB + c < 2):
                        pe.wait_ge(mix_read, i - 1)
                    pe.matmul(MB[r][0:TP, 0:D], xTs[:, r, 0, :], g.mixP[:, 0, :], start=True, stop=False)
                    pe.matmul(MB[r][0:TP, 0:D], xTs[:, r, 1, :], g.mixP[:, 1, :], start=False, stop=False)
                    pe.matmul(MB[r][0:TP, 0:D], g.ones[0:1, 0:TP], g.rows[0:1, 0:D], start=False, stop=True).then_inc(mix_ready, 1)

            def back(m, k, first):
                pe.wait_ge(xf_ready, m + 1)
                if not first:
                    pe.wait_ge(lg_read, m)
                for c in range(TB):
                    i = m * TB + c
                    r = (k * TB + c) % 2
                    if not (first and c < 2):
                        pe.wait_ge(xft_copied, i - 1)
                    for q in range(2):
                        u = pe.transpose(XB[r][:, q * 128:q * 128 + TP], xf[:, k, c, q * 128:(q + 1) * 128], g.ident[0:TP, 0:TP])
                    u.then_inc(xft_ready, 1)
                    pe.wait_ge(xft_copied, i + 1)
                    o = LB[0:TP, c * NE:(c + 1) * NE]
                    pe.matmul(o, xfT[:, r, 0, :], g.wrs[:, 0, :], start=True, stop=False)
                    pe.matmul(o, xfT[:, r, 1, :], g.wrs[:, 1, :], start=False, stop=False)
                    u = pe.matmul(o, g.ones[0:1, 0:TP], g.rows[0:1, D:D + NE], start=False, stop=True)
                u.then_inc(lg_ready, 1)
                pe.wait_ge(both_ready, m + 1)
                if not first:
                    pe.wait_ge(rank_read, m)
                pe.matmul(PB[0:TP, 0:TB * NE], g.ltb[0:TP, 0:TP], both[:, :, :], start=True, stop=False)
                for c in range(TB - 1):
                    u = pe.matmul(PB[0:TP, (c + 1) * NE:TB * NE], onesb[:, 0:TP],
                                  bc(both[:, c, :].unsqueeze(1), [TP, TB - 1 - c, NE]), start=False, stop=(c == TB - 2))
                u.then_inc(rank_ready, 1)
                pe.wait_ge(base_read, m + 1)
                for c in range(TB):
                    u = pe.matmul(RB[:, 0:NE], onesb[:, :], both[:, c, :], start=False, stop=True, skip_group_check=True)
                u.then_inc(total_ready, 1)

            front(0, 0, True)
            front(1, 1, True)
            back(0, 0, True)
            with pe.Fori(1, NBL // 2) as j:
                for k in range(2):
                    front(2 * j + k, k, False)
                    back(2 * j + (k - 1), 1 - k, False)
            back(NBL - 1, 1, False)

        @block.vector
        def _(v):
            v.memset(onesb[:, :], 1.0)
            v.tensor_scalar(ebase[:, :], g.iota[:, 0:NE], float(CAP), None, ALU.mult).then_inc(ebase_ready, 1)
            v.wait_ge(gb_in, 32)
            FL, BL = 6, 9

            def front(m, j, k, first):
                n = [0]

                def link(ins):
                    n[0] += 1
                    ins.then_inc(front_step, 1)
                    v.wait_ge(front_step, m * FL + n[0])
                v.wait_ge(sums_in[k], 16 * TB * (j + 1))
                s4 = sums[:, k, :, :].rearrange("p t (h f) -> p t h f", f=HW)
                link(v.tensor_scalar(den[:, :, :], s4[:, :, :, GF], 1e-16, None, ALU.max))
                link(v.reciprocal(rden[:, :, :], den[:, :, :]))
                if not first:
                    v.wait_ge(x2_out[k], 16 * j)
                th = x2[:, k, :, :].rearrange("p t (h f) -> p (t h) f", h=GH)
                ins = v.tensor_tensor(th, sums[:, k, :, :].rearrange("p t (h f) -> p (t h) f", f=HW)[:, :, 0:GF],
                                      bc(rden[:, :, :].rearrange("p t h -> p (t h)").unsqueeze(2), [TP, TB * GH, GF]), ALU.mult)
                ins.then_inc(sums_used, 1)
                v.wait_ge(sums_used, 2 * m + 1)
                v.wait_ge(x_in[k], 16 * (j + 1))
                v.tensor_tensor(x2[:, k, :, :], x2[:, k, :, :], xin[:, k, :, :], ALU.add).then_inc(sums_used, 1)
                v.wait_ge(sums_used, 2 * m + 2)
                for c in range(TB):
                    i = m * TB + c
                    v.wait_ge(mix_ready, i + 1)
                    v.tensor_tensor(x2[:, k, c, :], x2[:, k, c, :], MB[(k * TB + c) % 2][0:TP, 0:D], ALU.add).then_inc(mix_read, 1)
                for c in range(TB):
                    v.wait_ge(mix_read, m * TB + (c + 1))
                    ins = v.bn_stats(stats[:, c, :], x2[:, k, c, :])
                ins.then_inc(x2_ready, 1)
                after(v, g, x2_ready, m + 1)
                for c in range(TB):
                    ins = v.bn_aggr(mv[:, c, :], stats[:, c, :])
                link(ins)
                v.tensor_scalar(var2[:, :], mv[:, :, 1], 1.0 + EPS, EPS * EPS, ALU.mult, ALU.add).then_inc(var2_ready, 1)
                v.wait_ge(std2_ready, m + 1)
                link(v.reciprocal(r12[:, :], std2[:, :]))
                if not first:
                    v.wait_ge(sent[k], 32 * TB * j)
                    v.wait_ge(xft_ready, (m - 1) * TB)
                for c in range(TB):
                    ins = v.tensor_scalar(xf[:, k, c, :], x2[:, k, c, :], mv[:, c, 0:1], r12[:, c:c + 1], ALU.subtract, ALU.mult)
                link(ins)
                link(v.tensor_tensor(xf[:, k, :, :], xf[:, k, :, :], bc(gbc[:, :].unsqueeze(1), [TP, TB, D]), ALU.mult))
                v.tensor_tensor(xf[:, k, :, :], xf[:, k, :, :], bc(bbc[:, :].unsqueeze(1), [TP, TB, D]), ALU.add).then_inc(xf_ready, 1)
                assert n[0] == FL, n

            def back(m, j, k, first):
                n = [0]
                tiles = ds(m * TB, TB)

                def link(ins):
                    n[0] += 1
                    ins.then_inc(back_step, 1)
                    v.wait_ge(back_step, m * BL + n[0])
                v.wait_ge(lg_ready, m + 1)
                v.tensor_copy(lg[:, :, :], LB[0:TP, 0:TB * NE].rearrange("p (t e) -> p t e", e=NE)).then_inc(lg_read, 1)
                v.wait_ge(total_ready, m + 1)
                v.wait_ge(lg_read, m + 1)
                v.tensor_copy(base[:, :], RB[0:TP, 0:NE]).then_inc(base_read, 1)
                for c in range(TB):
                    ins = v.max(top[:, c, :], lg[:, c, :])
                link(ins)
                v.tensor_tensor(dl[:, :], top[:, :, 1], top[:, :, 0], ALU.subtract).then_inc(diff_ready, 1)
                for c in range(TB):
                    ins = v.max_index(topi[:, c, :], top[:, c, :], lg[:, c, :])
                link(ins)
                link(v.tensor_copy(topf[:, :, :], topi[:, :, :]))
                io = bc(g.iota[0:TP, 0:NE].unsqueeze(1), [TP, TB, NE])
                v.tensor_tensor(one1[:, :, :], io, bc(topf[:, :, 0:1], [TP, TB, NE]), ALU.is_equal)
                link(v.tensor_tensor(one2[:, :, :], io, bc(topf[:, :, 1:2], [TP, TB, NE]), ALU.is_equal))
                v.tensor_tensor(both[:, :, :], one1[:, :, :], one2[:, :, :], ALU.add).then_inc(both_ready, 1)
                v.tensor_copy(g.expert[:, :, tiles], topf[:, :, 0:2].rearrange("p t s -> p s t"))
                v.wait_ge(el_ready, m + 1)
                link(v.tensor_scalar(el1[:, :], el[:, :], 1.0, None, ALU.add))
                link(v.reciprocal(g.weight[:, 0, tiles], el1[:, :]))
                v.tensor_tensor(g.weight[:, 1, tiles], el[:, :], g.weight[:, 0, tiles], ALU.mult)
                v.wait_ge(rank_ready, m + 1)
                v.tensor_tensor(ranks[:, :, :], PB[0:TP, 0:TB * NE].rearrange("p (t e) -> p t e", e=NE),
                                bc(base[:, :].unsqueeze(1), [TP, TB, NE]), ALU.add).then_inc(rank_read, 1)
                v.wait_ge(rank_read, m + 1)
                v.tensor_tensor(pj[:, 0, :, :], ranks[:, :, :], one1[:, :, :], ALU.mult)
                link(v.tensor_tensor(pj[:, 1, :, :], ranks[:, :, :], one2[:, :, :], ALU.mult))
                link(v.tensor_reduce(pos[:, :, :], pj[:, :, :, :], axis=AX.X, op=ALU.add))
                link(v.tensor_copy(g.place[:, :, tiles], pos[:, :, :]))
                v.tensor_copy(posi[:, k, :, :], pos[:, :, :]).then_inc(pos_ready, 1)
                assert n[0] == BL, n

            front(0, 0, 0, True)
            front(1, 0, 1, True)
            back(0, 0, 0, True)
            with v.Fori(1, NBL // 2) as j:
                front(2 * j, j, 0, False)
                back(2 * j - 1, j - 1, 1, False)
                front(2 * j + 1, j, 1, False)
                back(2 * j, j, 0, False)
            back(NBL - 1, NBL // 2 - 1, 1, False)

            e = [0]

            def link(ins):
                e[0] += 1
                ins.then_inc(end_step, 1)
                v.wait_ge(end_step, e[0])
            v.wait_ge(total_ready, NBL + 1)
            v.wait_ge(ebase_ready, 1)
            link(v.tensor_reduce(prow[:, :], g.cst[:, C_LT:C_LT + 128], axis=AX.X, op=ALU.add))
            link(v.tensor_scalar(pcol[:, :], prow[:, :], -1.0, 127.0, ALU.mult, ALU.add))
            v.tensor_scalar(padi[:, :], RB[:, 0:NE], pcol[:, 0:1], None, ALU.add).then_inc(pad_ready, 1)
            link(v.tensor_tensor(cnts[:, :], RB[:, 0:NE], ebase[:, :], ALU.subtract))
            link(v.tensor_scalar(cnti[:, :], cnts[:, :], 127.0, None, ALU.add))
            link(v.tensor_scalar(cntj[:, :], cnti[:, :], 7, None, ALU.arith_shift_right))
            link(v.tensor_copy(nch[:, :], cntj[:, :]))
            link(v.tensor_tensor_scan(ends[:, :], nch[:, :], g.zero[:, 0:NE], 0.0, ALU.add, ALU.add))
            link(v.tensor_tensor(begin[:, :], ends[:, :], nch[:, :], ALU.subtract))
            link(v.tensor_scalar(last[:, :], ends[:, NE - 1:NE], -1.0, None, ALU.add))
            link(v.tensor_scalar(chc[:, :], g.iota[0:1, 0:MC], last[0:1, 0:1], None, ALU.min))
            for q in range(NE - 1):
                v.tensor_scalar(past[:, q, :], chc[:, :], ends[0:1, q:q + 1], None, ALU.is_ge)
                ins = v.tensor_scalar(pastn[:, q, :], chc[:, :], ends[0:1, q:q + 1], nch[0:1, q:q + 1], ALU.is_ge, ALU.mult)
            link(ins)
            v.tensor_reduce(ex[:, :], past[:, :, :].rearrange("p q c -> p c q"), axis=AX.X, op=ALU.add)
            link(v.tensor_reduce(bg[:, :], pastn[:, :, :].rearrange("p q c -> p c q"), axis=AX.X, op=ALU.add))
            link(v.tensor_tensor(df[:, :], chc[:, :], bg[:, :], ALU.subtract))
            link(v.tensor_scalar(rw[:, :], df[:, :], 128.0, None, ALU.mult))
            v.scalar_tensor_tensor(g.chunk_row[:, :], ex[:, :], float(CAP), rw[:, :], ALU.mult, ALU.add)
            v.tensor_copy(g.chunk_expert[:, :], ex[:, :])
            link(v.scalar_tensor_tensor(delta[:, :], begin[:, :], 128.0, ebase[:, :], ALU.mult, ALU.subtract))
            own = g.expert[:, :, :].rearrange("p s t -> p (s t)")
            for q in range(NE):
                ins = v.tensor_scalar(yd[:, q, :], own, float(q), delta[0:TP, q:q + 1], ALU.is_equal, ALU.mult)
            link(ins)
            link(v.tensor_tensor(yacc[:, 0, :], g.place[:, :, :].rearrange("p s t -> p (s t)"), yd[:, 0, :], ALU.add))
            for q in range(1, NE):
                link(v.tensor_tensor(yacc[:, q, :], yacc[:, q - 1, :], yd[:, q, :], ALU.add))
            v.tensor_copy(g.yidx[:, :, :].rearrange("p s t -> p (s t)"), yacc[:, NE - 1, :])


def expert_loop(nc, g):
    with ExitStack() as ctx:
        t = Parts(nc, ctx, "expert")
        sb, sem, sems = t.sb, t.sem, t.sems
        xs, xsT = sb("xs", [128, 2, D]), sb("xsT", [128, 2, 2, 128])
        b1bc, b2bc = sb("b1bc", [128, NE, HID]), sb("b2bc", [128, NE, D])
        hb, hg, hT = sb("hb", [128, 2, HID]), sb("hg", [128, 2, HID]), sb("hT", [128, 2, HID])
        y = sb("y", [128, 2, D])
        b_in, xs_in, y_out = sem("b_in"), sems("xs_in", 2), sems("y_out", 2)
        xt_ready, xt_copied, h_ready, hb_ready = sem("ext_ready"), sem("ext_copied"), sem("eh_ready"), sem("hb_ready")
        hg_ready, ht_ready, ht_copied, y_made, y_ready = sem("hg_ready"), sem("ht_ready"), sem("ht_copied"), sem("y_made"), sem("y_ready")
        block = ctx.enter_context(nc.Block())
        b = g.bank
        XB, HB, TBK, YB = b[0:2], b[2:4], b[4:6], b[6:8]
        HALFC = MC // 2

        def experts(eng, j):
            first, last = isinstance(j, int) and j == 0, isinstance(j, int) and j == HALFC
            c0, n = (0 if first else 2 * j - 2), (2 if first or last else 4)
            _, e = nc.values_load_multi_w_load_instructions(g.chunk_expert[0:1, ds(c0, n)], engines=(eng.engine,),
                                                            min_val=0, max_val=NE - 1)
            return (None, None) * first + tuple(e)

        def pairs(eng, step):
            for j in range(2):
                step(j, experts(eng, j))
            with eng.Fori(2, HALFC - 1) as j:
                step(j, experts(eng, j))
            step(HALFC - 1, experts(eng, HALFC - 1))

        def wait(eng, sem, value):
            if not isinstance(value, int) or value > 0:
                eng.wait_ge(sem, value)

        def exists(c):
            return not isinstance(c, int) or 0 <= c < MC

        @block.sync
        def _(sp):
            sp.dma_start(b1bc[:, :, :], g.b1.rearrange("e h -> (e h)").partition_broadcast(128).rearrange("p (e h) -> p e h", e=NE)).then_inc(b_in, 16)
            sp.dma_start(b2bc[:, :, :], g.b2.rearrange("e h -> (e h)").partition_broadcast(128).rearrange("p (e h) -> p e h", e=NE)).then_inc(b_in, 16)

            def step(j, first):
                for k in range(2):
                    c = 2 * j + k
                    row = sp.value_load(g.chunk_row[0:1, ds(c, 1)], min_val=0, max_val=NE * CAP - 128)
                    if not first:
                        sp.wait_ge(xt_ready, c - 1)
                    sp.dma_start(xs[:, k, :], g.xs_d[ds(row, 128), :]).then_inc(xs_in[k], 16)
            step(0, True)
            with sp.Fori(1, HALFC) as j:
                step(j, False)

        @block.gpsimd
        def _(pool):
            with pool.Fori(0, HALFC) as j:
                for k in range(2):
                    c = 2 * j + k
                    pool.wait_ge(y_ready, c + 1)
                    pool.dma_start(g.ys_d[ds(c * 128, 128), :], y[:, k, :]).then_inc(y_out[k], 16)
            for k in range(2):
                pool.wait_ge(y_out[k], 16 * HALFC)

        @block.tensor
        def _(pe):
            def turn_x(c, k, use):
                pe.wait_ge(xs_in[k], 16 * use)
                wait(pe, xt_copied, c - 1)
                for q in range(2):
                    u = pe.transpose(XB[k][:, q * 128:(q + 1) * 128], xs[:, k, q * 128:(q + 1) * 128], g.ident)
                u.then_inc(xt_ready, 1)

            def hidden(c, k, e):
                pe.wait_ge(xt_copied, c + 1)
                wait(pe, hb_ready, c - 1)
                for q in range(2):
                    u = pe.matmul(HB[k][:, :], xsT[:, k, q, :], g.w1s[:, ds(e, 1), q, :].rearrange("p a f -> p (a f)"), start=(q == 0), stop=(q == 1))
                u.then_inc(h_ready, 1)

            def turn_h(c, k):
                pe.wait_ge(hg_ready, c + 1)
                wait(pe, ht_copied, c - 1)
                for q in range(4):
                    u = pe.transpose(TBK[k][:, q * 128:(q + 1) * 128], hg[:, k, q * 128:(q + 1) * 128], g.ident)
                u.then_inc(ht_ready, 1)

            def output(c, k, e):
                pe.wait_ge(ht_copied, c + 1)
                wait(pe, y_ready, c - 1)
                for q in range(4):
                    u = pe.matmul(YB[k][:, 0:D], hT[:, k, q * 128:(q + 1) * 128], g.w2s[:, ds(e, 1), q, :].rearrange("p a f -> p (a f)"), start=(q == 0), stop=(q == 3))
                u.then_inc(y_made, 1)

            def step(j, e):
                for k in range(2):
                    c = 2 * j + k
                    hidden(c, k, e[2 + k])
                    if exists(c + 1):
                        turn_x(c + 1, 1 - k, j + 1 + k)
                    if exists(c - 1):
                        turn_h(c - 1, 1 - k)
                    if exists(c - 2):
                        output(c - 2, k, e[k])
            turn_x(0, 0, 1)
            pairs(pe, step)
            e = experts(pe, HALFC)
            turn_h(MC - 1, 1)
            output(MC - 2, 0, e[0])
            output(MC - 1, 1, e[1])

        @block.scalar
        def _(act):
            def copy_x(c, k):
                act.wait_ge(xt_ready, c + 1)
                wait(act, h_ready, c - 1)
                act.copy(xsT[:, k, :, :], XB[k][:, 0:D].rearrange("p (q n) -> p q n", q=2)).then_inc(xt_copied, 1)

            def gelu(c, k):
                act.wait_ge(hb_ready, c + 1)
                wait(act, ht_ready, c - 1)
                act.activation(hg[:, k, :], hb[:, k, :], ACT.Gelu).then_inc(hg_ready, 1)

            def step(j):
                for k in range(2):
                    c = 2 * j + k
                    if exists(c + 1):
                        copy_x(c + 1, 1 - k)
                    gelu(c, k)
            copy_x(0, 0)
            for j in range(2):
                step(j)
            with act.Fori(2, HALFC - 1) as j:
                step(j)
            step(HALFC - 1)

        @block.vector
        def _(v):
            v.wait_ge(b_in, 32)

            def bias(c, k, e):
                v.wait_ge(h_ready, c + 1)
                wait(v, hg_ready, c - 1)
                v.tensor_tensor(hb[:, k, :], HB[k][:, :], b1bc[:, ds(e, 1), :].rearrange("p a f -> p (a f)"), ALU.add).then_inc(hb_ready, 1)

            def copy_h(c, k):
                v.wait_ge(ht_ready, c + 1)
                wait(v, y_made, c - 1)
                v.tensor_copy(hT[:, k, :], TBK[k][:, :]).then_inc(ht_copied, 1)

            def result(c, k, e, uses):
                v.wait_ge(y_made, c + 1)
                wait(v, y_out[k], 16 * uses)
                v.tensor_tensor(y[:, k, :], YB[k][:, 0:D], b2bc[:, ds(e, 1), :].rearrange("p a f -> p (a f)"), ALU.add).then_inc(y_ready, 1)

            def step(j, e):
                for k in range(2):
                    c = 2 * j + k
                    bias(c, k, e[2 + k])
                    if exists(c - 1):
                        copy_h(c - 1, 1 - k)
                    if exists(c - 2):
                        result(c - 2, k, e[k], j - 1)
            pairs(v, step)
            e = experts(v, HALFC)
            copy_h(MC - 1, 1)
            result(MC - 2, 0, e[0], HALFC - 1)
            result(MC - 1, 1, e[1], HALFC - 1)


def combine_loop(nc, g):
    with ExitStack() as ctx:
        t = Parts(nc, ctx, "combine")
        sb, sem, sems = t.sb, t.sem, t.sems
        idx = sb("cidx", [TP, 2, 2, TB], I32)
        x2, ys = sb("cx2", [TP, 2, TB, D]), sb("cys", [TP, 2, 2, TB, D])
        o1, o2 = sb("o1", [TP, 2, TB, D]), sb("o2", [TP, 2, TB, D])
        idx_ready, ys_in, x2_in, out_done = sem("cidx_ready"), sems("ys_in", 2), sems("x2_in", 2), sems("out_done", 2)
        o1_ready, o2_ready = sem("o1_ready"), sem("o2_ready")
        block = ctx.enter_context(nc.Block())

        def view(ap, m):
            return ap[ds(m * (TB * TP), TB * TP), :].rearrange("(t p) f -> p t f", p=TP)

        def blocks(eng, step):
            for k in range(2):
                step(k, 0, k, True)
            with eng.Fori(1, NBL // 2) as j:
                for k in range(2):
                    step(2 * j + k, j, k, False)

        @block.sync
        def _(sp):
            def step(m, j, k, first):
                if not first:
                    sp.wait_ge(o1_ready, m - 1)
                sp.dma_start(x2[:, k, :, :], view(g.x2_d, m)).then_inc(x2_in[k], 16)
            blocks(sp, step)

        @block.scalar
        def _(act):
            def step(m, j, k, first):
                act.wait_ge(o2_ready, m + 1)
                act.dma_start(view(g.out, m), o2[:, k, :, :]).then_inc(out_done[k], 16)
            blocks(act, step)
            for k in range(2):
                act.wait_ge(out_done[k], 16 * (NBL // 2))

        @block.gpsimd
        def _(pool):
            def step(m, j, k, first):
                if not first:
                    pool.wait_ge(ys_in[k], 32 * TB * j)
                pool.tensor_copy(idx[:, k, :, :], g.yidx[:, :, ds(m * TB, TB)]).then_inc(idx_ready, 1)
                if not first:
                    pool.wait_ge(o2_ready, m - 1)
                after(pool, g, idx_ready, m + 1)
                for c in range(TB):
                    for s in range(2):
                        pool.indirect_dma_start(ys[:, k, s, c, :], None, g.ys_d,
                                                bass.IndirectOffsetOnAxis(ap=idx[:, k, s, c:c + 1], axis=0)).then_inc(ys_in[k], 16)
            blocks(pool, step)

        @block.vector
        def _(v):
            def step(m, j, k, first):
                v.wait_ge(x2_in[k], 16 * (j + 1))
                v.wait_ge(ys_in[k], 32 * TB * (j + 1))
                for c in range(TB):
                    i = v.scalar_tensor_tensor(o1[:, k, c, :], ys[:, k, 0, c, :], g.weight[:, 0, ds(m * TB + c, 1)], x2[:, k, c, :], ALU.mult, ALU.add)
                i.then_inc(o1_ready, 1)
                v.wait_ge(o1_ready, m + 1)
                if not first:
                    v.wait_ge(out_done[k], 16 * j)
                for c in range(TB):
                    i = v.scalar_tensor_tensor(o2[:, k, c, :], ys[:, k, 1, c, :], g.weight[:, 1, ds(m * TB + c, 1)], o1[:, k, c, :], ALU.mult, ALU.add)
                i.then_inc(o2_ready, 1)
            blocks(v, step)


class Shared:
    pass


def program(nc, ins, out):
    g = Shared()
    (g.x, g.src, g.dst, g.gW, g.gal, g.gar, g.wqkv, g.wout, g.bout, g.gamma, g.beta, g.wr, g.br,
     g.w1, g.b1, g.w2, g.b2, g.const) = ins
    g.out = out

    def dram(name, shape, dt=F32):
        return nc.dram_tensor(name, shape, dt, kind="Internal").ap()

    g.hist_d = dram("hist_d", (2, HI * LO))
    g.cols_d = dram("cols_d", (2, NB))
    g.sorted_d = dram("sorted_d", (128 * NCH, 1), I32)
    g.table_d = dram("table_d", (N, ROW))
    g.hl_d = dram("hl_d", (NB * BR, GH))
    g.sums_d = dram("sums_d", (NCH * BR, TW))
    g.node_d = dram("node_d", (NB * BR, 1), I32)
    g.x2_d = dram("x2_d", (N, D))
    g.xs_d = dram("xs_d", (NE * CAP, D))
    g.ys_d = dram("ys_d", (MC * 128, D))
    with ExitStack() as ctx:
        t = Parts(nc, ctx, "all")
        sb = t.sb
        g.bank = [ctx.enter_context(nc.psum_tensor(f"bank{n}", [128, 512], F32)) for n in range(8)]
        g.late_in, g.filled = t.sem("late_in"), t.sem("filled")
        g.passed = t.sem("passed")
        g.cst = sb("cst", [128, CW])
        g.ident, g.iota = g.cst[:, C_ID:C_ID + 128], g.cst[:, C_IO:C_IO + NCH]
        g.ltb, g.geb = sb("ltb", [128, 128], BF16), sb("geb", [128, 128], BF16)
        g.iotab = sb("iotab", [128, NB], BF16)
        g.eps = sb("eps", [128, 1])
        g.ones, g.zero = sb("ones", [128, 128]), sb("zeros", [128, 512])
        g.rows = sb("rows", [1, D + NE])
        g.wrs = sb("wrs", [128, 2, NE])
        g.w1s, g.w2s = sb("w1s", [128, NE, 2, HID]), sb("w2s", [128, NE, 4, D])
        g.nodeidx = sb("nodeidx", [TP, NT], I32)
        g.mixP = sb("mixP", [128, 2, D])
        g.weight, g.expert, g.place = sb("weight", [TP, 2, NT]), sb("expert", [TP, 2, NT]), sb("place_", [TP, 2, NT])
        g.yidx = sb("yidx", [TP, 2, NT], I32)
        g.chunk_row, g.chunk_expert = sb("chunk_row", [1, MC], I32), sb("chunk_expert", [1, MC], I32)
        with ExitStack() as c2:
            t2 = Parts(nc, c2, "x")
            g.xnT = t2.sb("xnT", [128, NT, 2, TP])
            with ExitStack() as c3:
                t3 = Parts(nc, c3, "mix")
                g.woT, g.wq = t3.sb("woT", [128, 4, D]), t3.sb("wq", [128, 4, D])
                with ExitStack() as c4:
                    t4 = Parts(nc, c4, "node0")
                    g.wa = t4.sb("wa", [128, 2, D + 2 * GH])
                    g.wkvT = t4.sb("wkvT", [128, 2, 2 * INNER])
                    g.firsts = t4.sb("firsts", [128, 2, NB])
                    g.bktf, g.packi = t4.sb("bktf", [TP, EC]), t4.sb("packi", [TP, EC], I32)
                    setup(nc, g)
                    node_loop(nc, g)
                g.hlc, g.reset = t3.sb("hlc", [128, NCH]), t3.sb("reset", [128, NCH])
                g.local, g.colidx = t3.sb("local", [128, NCH]), t3.sb("colidx", [128, NCH], I32)
                chunk_tables(nc, g)
                edge_loop(nc, g)
            token_loop(nc, g)
        expert_loop(nc, g)
        combine_loop(nc, g)


_INS = ["x", "src", "dst", "L0_gnn_W", "L0_gnn_a_l", "L0_gnn_a_r", "L0_mix_Wqkv", "L0_mix_Wout", "L0_mix_bout",
        "L0_ffn_gamma", "L0_ffn_beta", "L0_ffn_Wr", "L0_ffn_br", "L0_ffn_W1", "L0_ffn_b1", "L0_ffn_W2", "L0_ffn_b2"]


def kernel(**inputs):
    import numpy as np
    import concourse.bacc as bacc
    from concourse.bass_utils import run_bass_kernel_spmd

    nc = bacc.Bacc("TRN2", target_bir_lowering=False, num_devices=1)
    arrays = {f"in_{n}": np.ascontiguousarray(inputs[n]) for n in _INS}
    arrays["in_const"] = constants()
    ins = [nc.dram_tensor(n, a.shape, mybir.dt.from_np(a.dtype), kind="ExternalInput").ap() for n, a in arrays.items()]
    out = nc.dram_tensor("out", (N, D), F32, kind="ExternalOutput").ap()
    program(nc, ins, out)
    r = run_bass_kernel_spmd(nc, [arrays], core_ids=[0])
    return r.results[0]["out"]
```

```python
from contextlib import ExitStack

import concourse.bass as bass
from concourse import mybir
from concourse.alu_op_type import AluOpType as ALU

F32, I32, U32, BF16 = mybir.dt.float32, mybir.dt.int32, mybir.dt.uint32, mybir.dt.bfloat16
ACT = mybir.ActivationFunctionType
AX = mybir.AxisListType
ds = bass.ds

N, D = 6250, 256
EDGES = 100000
GH, GF = 4, 64
SLOPE = 0.2
MH, MF = 8, 64
INNER = MH * MF
NE, HID = 8, 512
EPS = 1e-5
TP, NT = 125, 50
EC = EDGES // TP
EK = EC // NT
HALF = EC // 2
HK = 20
BR = 32
NB = -(-N // BR)
HI, LO = -(-NB // 16), 16
NBT = NB // 2
GU = 4
RING = 6
NCH = -(-((EDGES + NB * 128) // 128) // (GU * RING)) * GU * RING
NG = NCH // GU
HW = GF + 1
TW = GH * HW
ROW = TW + GH
BIG, FLOOR = 1e30, 1e28
COLBITS = 13
PAD = BR << COLBITS
TB = 5
NBL = NT // TB
CAP = N + 128
C_B, C_W2, C_MN, C_DW, C_E1 = (D + n for n in range(5))
XW = D + 5
MC = -(-((2 * N + NE * 127) // 128) // 2) * 2
C_ID, C_LT, C_IO = 0, 128, 256
CW = C_IO + NCH


def constants():
    import numpy as np
    c = np.zeros((128, CW), np.float32)
    p = np.arange(128)
    c[:, C_ID:C_ID + 128] = np.eye(128)
    c[:, C_LT:C_LT + 128] = p[:, None] < p[None, :]
    c[:, C_IO:] = np.arange(NCH)
    return c


def bc(ap, shape):
    return ap.to_broadcast(shape)


def after(eng, g, sem, value):
    eng.wait_ge(sem, value)
    eng.sem_inc(g.passed, 1)


class Parts:

    def __init__(self, nc, ctx, stage):
        self.nc, self.ctx, self.stage, self.sems_held = nc, ctx, stage, []
        ctx.callback(self.clear)

    def clear(self):
        if self.sems_held:
            self.nc.clear_and_free_semaphores(self.sems_held)
            self.nc.all_engine_barrier()

    def sb(self, name, shape, dt=F32):
        return self.ctx.enter_context(self.nc.sbuf_tensor(f"{self.stage}_{name}", shape, dt))

    def sem(self, name):
        self.sems_held.append(self.nc.alloc_semaphore(name=f"{self.stage}_{name}"))
        return self.sems_held[-1]

    def sems(self, name, n):
        return [self.sem(f"{name}{k}") for k in range(n)]


def setup(nc, g):
    with ExitStack() as ctx:
        t = Parts(nc, ctx, "setup")
        sb, sem = t.sb, t.sem
        room = g.xnT[0:TP, :, :, :].rearrange("p t q n -> p (t q n)")
        hif, lof, *ints = (room[:, n * EC:(n + 1) * EC] for n in range(8))
        srcs, dsts, bkti, hii, loi, pk1 = (r.bitcast(I32) for r in ints)
        oneh = sb("oneh", [TP, 2, HK, HI + LO], BF16)
        zerob = sb("zerob", [TP, HI + LO], BF16)
        hists = sb("hists", [HI, 2, LO])
        cnt = sb("cnt", [128, 2, HI * LO])
        tot, toti = sb("tot", [128, NB]), sb("toti", [128, NB], I32)
        totj, chk = sb("totj", [128, NB], I32), sb("chk", [128, NB])
        zero, endc, firstc = sb("zero", [128, NB]), sb("endc", [128, NB]), sb("firstc", [128, NB])
        padt = sb("padt", [128, NCH], I32)
        zhl = sb("zhl", [NB * BR - N, GH])
        abc = sb("abc", [128, 2, D])
        wprod = sb("wprod", [128, 2, 2, D])
        wkvn = sb("wkvn", [128, 8, D])
        wmean = sb("wmean", [128, 2, 2 * MH])
        won = sb("won", [128, 2, INNER])

        const_in, edge_in, w_in, a_in = sem("const_in"), sem("edge_in"), sem("w_in"), sem("a_in")
        kv_in, wo_in = sem("kv_in"), sem("wo_in")
        ones_ready = sem("ones_ready")
        ints_ready, digit_ready = sem("ints_ready"), sem("digit_ready")
        fill_ready = sem("fill_ready")
        oneh_ready, oneh_used = sem("oneh_ready"), sem("oneh_used")
        hist_done, hist_copied, hist_out, cnt_in = (sem("hist_done"), sem("hist_copied"),
                                                    sem("hist_out"), sem("cnt_in"))
        step, cols_ready, cols_out = sem("table_step"), sem("cols_ready"), sem("cols_out")
        wt_done, wt_copied = sem("wt_done"), sem("wt_copied")
        mean_ready, prod_ready, a_ready = sem("mean_ready"), sem("prod_ready"), sem("a_ready")
        block = ctx.enter_context(nc.Block())
        b = g.bank

        @block.sync
        def _(sp):
            sp.dma_start(g.cst[:, :], g.const).then_inc(const_in, 16)
            sp.dma_start(srcs[:, :], g.src.rearrange("(p c) -> p c", p=TP)).then_inc(edge_in, 16)
            sp.dma_start(dsts[:, :], g.dst.rearrange("(p c) -> p c", p=TP)).then_inc(edge_in, 16)
            sp.dma_start(wkvn[:, :, :], g.wqkv[INNER:3 * INNER, :].rearrange("(s p) c -> p s c", p=128)).then_inc(kv_in, 16)
            sp.dma_start(won[:, :, :], g.wout.rearrange("(s p) f -> p s f", p=128)).then_inc(wo_in, 16)
            sp.dma_start(g.wa[:, :, 0:D], g.gW.rearrange("(k p) f -> p k f", p=128)).then_inc(w_in, 16)
            sp.dma_start(abc[:, 0, :], g.gar.rearrange("a h f -> a (h f)").partition_broadcast(128)).then_inc(a_in, 16)
            sp.dma_start(abc[:, 1, :], g.gal.rearrange("a h f -> a (h f)").partition_broadcast(128)).then_inc(a_in, 16)
            sp.dma_start(g.wq[:, :, :], g.wqkv[0:INNER, :].rearrange("(s p) c -> p s c", p=128)).then_inc(g.late_in, 16)
            sp.dma_start(g.wrs[:, :, :], g.wr.rearrange("(k p) e -> p k e", p=128)).then_inc(g.late_in, 16)
            for e in range(NE):
                sp.dma_start(g.w1s[:, e, :, :], g.w1[e].rearrange("(k p) h -> p k h", p=128)).then_inc(g.late_in, 16)
                sp.dma_start(g.w2s[:, e, :, :], g.w2[e].rearrange("(k p) h -> p k h", p=128)).then_inc(g.late_in, 16)
            sp.wait_ge(fill_ready, 2)
            sp.dma_start(g.sorted_d.rearrange("(p c) a -> p (c a)", p=128), padt[:, :]).then_inc(g.filled, 16)
            sp.dma_start(g.hl_d[N:NB * BR, :], zhl[:, :]).then_inc(g.filled, 16)
            sp.wait_ge(hist_copied, 2)
            sp.dma_start(g.hist_d.rearrange("s (h l) -> h s l", l=LO), hists[:, :, :]).then_inc(hist_out, 16)
            sp.wait_ge(hist_out, 16)
            sp.dma_start(cnt[:, :, :], g.hist_d.rearrange("s b -> (s b)").partition_broadcast(128).rearrange("p (s b) -> p s b", s=2)).then_inc(cnt_in, 16)
            sp.wait_ge(cols_ready, 2)
            sp.dma_start(g.cols_d[0:1, :], firstc[0:1, :]).then_inc(cols_out, 16)
            sp.dma_start(g.cols_d[1:2, :], endc[0:1, :]).then_inc(cols_out, 16)
            sp.wait_ge(cols_out, 32)
            sp.wait_ge(g.filled, 32)
            sp.wait_ge(g.late_in, 16 * (2 + 2 * NE))

        @block.gpsimd
        def _(pool):
            pool.memset(padt[:, :], PAD).then_inc(fill_ready, 1)
            pool.memset(zhl[:, :], 0.0).then_inc(fill_ready, 1)

        @block.vector
        def _(v):
            v.memset(g.ones[:, :], 1.0).then_inc(ones_ready, 1)
            v.memset(zerob[:, :], 0.0).then_inc(ones_ready, 1)
            v.memset(zero[:, :], 0.0)
            v.memset(g.eps[:, :], EPS)
            v.memset(g.zero[:, :], 0.0).then_inc(ones_ready, 1)
            v.wait_ge(edge_in, 32)
            v.tensor_scalar(bkti[:, :], srcs[:, :], 5, None, ALU.arith_shift_right).then_inc(ints_ready, 1)
            v.tensor_scalar(hii[:, :], srcs[:, :], 9, None, ALU.arith_shift_right).then_inc(ints_ready, 1)
            v.tensor_scalar(loi[:, :], srcs[:, :], 5, LO - 1, ALU.arith_shift_right, ALU.bitwise_and).then_inc(ints_ready, 1)
            v.tensor_scalar(pk1[:, :], srcs[:, :], BR - 1, COLBITS, ALU.bitwise_and, ALU.logical_shift_left).then_inc(ints_ready, 1)
            v.wait_ge(ints_ready, 4)
            v.tensor_copy(hif[:, :], hii[:, :]).then_inc(digit_ready, 1)
            v.tensor_copy(lof[:, :], loi[:, :]).then_inc(digit_ready, 1)
            v.tensor_copy(g.bktf[:, :], bkti[:, :])
            v.tensor_tensor(g.packi[:, :], pk1[:, :], dsts[:, :], ALU.bitwise_or)
            v.wait_ge(const_in, 16)
            v.wait_ge(digit_ready, 2)
            iota = g.iota[0:TP, :]

            def digits(j, first):
                for k in range(2):
                    if not first:
                        v.wait_ge(oneh_used, 2 * j + k - 1)
                    c0 = (2 * j + k) * HK
                    v.tensor_tensor(oneh[:, k, :, 0:HI], bc(hif[:, ds(c0, HK)].unsqueeze(2), [TP, HK, HI]),
                                    bc(iota[:, 0:HI].unsqueeze(1), [TP, HK, HI]), ALU.is_equal).then_inc(oneh_ready, 1)
                    v.tensor_tensor(oneh[:, k, :, HI:HI + LO], bc(lof[:, ds(c0, HK)].unsqueeze(2), [TP, HK, LO]),
                                    bc(iota[:, 0:LO].unsqueeze(1), [TP, HK, LO]), ALU.is_equal).then_inc(oneh_ready, 1)
            digits(0, True)
            with v.Fori(1, EC // HK // 2) as j:
                digits(j, False)
            v.tensor_copy(g.ltb[:, :], g.cst[:, C_LT:C_LT + 128])
            v.tensor_scalar(g.geb[:, :], g.cst[:, C_LT:C_LT + 128], -1.0, 1.0, ALU.mult, ALU.add)
            v.tensor_copy(g.iotab[:, :], g.iota[:, 0:NB])
            v.wait_ge(hist_done, 2)
            for s in range(2):
                v.tensor_copy(hists[:, s, :], b[s][0:HI, 0:LO]).then_inc(hist_copied, 1)
            v.wait_ge(w_in, 16)
            v.wait_ge(a_in, 32)
            for k in range(2):
                for s in range(2):
                    v.tensor_tensor(wprod[:, k, s, :], g.wa[:, k, 0:D], abc[:, s, :], ALU.mult).then_inc(prod_ready, 1)
            v.wait_ge(prod_ready, 4)
            for k in range(2):
                for s in range(2):
                    v.tensor_reduce(g.wa[:, k, D + s * GH:D + (s + 1) * GH],
                                    wprod[:, k, s, :].rearrange("p (h f) -> p h f", h=GH), axis=AX.X, op=ALU.add)
            n = [0]

            def link(ins):
                n[0] += 1
                ins.then_inc(step, 1)
                v.wait_ge(step, n[0])
            v.wait_ge(cnt_in, 16)
            link(v.tensor_tensor(tot[:, :], cnt[:, 0, 0:NB], cnt[:, 1, 0:NB], ALU.add))
            link(v.tensor_scalar(toti[:, :], tot[:, :], 127.0, None, ALU.add))
            link(v.tensor_scalar(totj[:, :], toti[:, :], 7, None, ALU.arith_shift_right))
            link(v.tensor_scalar(chk[:, :], totj[:, :], 1.0, None, ALU.max))
            v.tensor_tensor_scan(endc[:, :], chk[:, :], zero[:, :], 0.0, ALU.add, ALU.add).then_inc(cols_ready, 1)
            v.wait_ge(cols_ready, 1)
            v.tensor_tensor(firstc[:, :], endc[:, :], chk[:, :], ALU.subtract).then_inc(cols_ready, 1)
            v.wait_ge(cols_ready, 2)
            link(v.tensor_scalar(g.firsts[:, 0, :], firstc[:, :], 128.0, None, ALU.mult))
            link(v.tensor_tensor(g.firsts[:, 1, :], g.firsts[:, 0, :], cnt[:, 0, 0:NB], ALU.add))
            v.wait_ge(wt_copied, 6)
            for k in range(2):
                v.tensor_reduce(wmean[:, k, :], g.wkvT[:, k, :].rearrange("p (h f) -> p h f", f=MF),
                                axis=AX.X, op=ALU.add).then_inc(mean_ready, 1)
            v.wait_ge(mean_ready, 2)
            for k in range(2):
                w = g.wkvT[:, k, :].rearrange("p (h f) -> p h f", f=MF)
                v.scalar_tensor_tensor(w, bc(wmean[:, k, :].unsqueeze(2), [128, 2 * MH, MF]), -1.0 / MF, w,
                                       ALU.mult, ALU.add)

        @block.tensor
        def _(pe):
            pe.wait_ge(ones_ready, 2)
            for s in range(2):
                pe.matmul(b[s][0:HI, 0:LO], zerob[:, 0:HI], zerob[:, HI:HI + LO], start=True, stop=True)
            steps = EC // HK // 2
            for s in range(2):
                with pe.Fori(s * steps // 2, (s + 1) * steps // 2) as j:
                    for k in range(2):
                        pe.wait_ge(oneh_ready, 4 * j + 2 * k + 2)
                        for c in range(HK):
                            m = pe.matmul(b[s][0:HI, 0:LO], oneh[:, k, c, 0:HI], oneh[:, k, c, HI:HI + LO],
                                          start=False, stop=True, skip_group_check=True)
                        m.then_inc(oneh_used, 1)
            pe.matmul(b[0][0:HI, 0:LO], zerob[:, 0:HI], zerob[:, HI:HI + LO], start=False, stop=True, skip_group_check=True).then_inc(hist_done, 1)
            pe.matmul(b[1][0:HI, 0:LO], zerob[:, 0:HI], zerob[:, HI:HI + LO], start=False, stop=True, skip_group_check=True).then_inc(hist_done, 1)
            pe.wait_ge(const_in, 16)
            pe.wait_ge(kv_in, 16)
            for k in range(2):
                for s in range(8):
                    m = pe.transpose(b[2 + 2 * k + s // 4][:, (s % 4) * 128:(s % 4 + 1) * 128],
                                     wkvn[:, s, k * 128:(k + 1) * 128], g.ident)
                    if s % 4 == 3:
                        m.then_inc(wt_done, 1)
            pe.wait_ge(wo_in, 16)
            for q in range(4):
                for s in range(2):
                    m = pe.transpose(b[6 + q // 2][:, (q % 2) * 256 + s * 128:(q % 2) * 256 + (s + 1) * 128],
                                     won[:, s, q * 128:(q + 1) * 128], g.ident)
                if q % 2:
                    m.then_inc(wt_done, 1)

        @block.scalar
        def _(act):
            for k in range(2):
                for hf in range(2):
                    act.wait_ge(wt_done, 2 * k + hf + 1)
                    act.copy(g.wkvT[:, k, hf * 512:(hf + 1) * 512], b[2 + 2 * k + hf][:, :]).then_inc(wt_copied, 1)
            for q in range(2):
                act.wait_ge(wt_done, 5 + q)
                act.copy(g.woT[:, 2 * q:2 * q + 2, :], b[6 + q][:, :].rearrange("p (q c) -> p q c", q=2)).then_inc(wt_copied, 1)


def node_loop(nc, g):
    with ExitStack() as ctx:
        t = Parts(nc, ctx, "node")
        sb, sem, sems = t.sb, t.sem, t.sems
        S = EK // 2
        onehot = sb("onehot", [TP, 2, S, NB], BF16)
        junk = sb("junk", [TP, 2, NB])
        place = sb("place", [TP, EK])
        placei, slot = sb("placei", [TP, EK], I32), sb("slot", [TP, EK], I32)
        chunk = sb("chunk", [TP, EK], I32)
        where, load = sb("where", [TP, 2, EK], I32), sb("load", [TP, 2, EK], I32)
        xin = sb("xin", [TP, 2, D])
        stats, mv = sb("stats", [TP, 6]), sb("mv", [TP, 2])
        std, rstd = sb("std", [TP, 1]), sb("rstd", [TP, 1])
        kstd = sb("kstd", [TP, 2 * MH])
        xn = sb("xn", [TP, 2, D])
        xT = sb("xT", [128, 2, 2, TP])
        tab = sb("tab", [TP, 2, ROW])
        hlt = sb("hlt", [TP, 2, GH])
        kc, vc = sb("kc", [TP, 2, INNER]), sb("vc", [TP, 2, INNER])
        sq = sb("sq", [TP, 2, 2 * INNER])
        var, kvr, vs = sb("var", [TP, 2 * MH]), sb("kvr", [TP, 2 * MH]), sb("vs", [TP, 2, INNER])
        scl = sb("scl", [TP, MH])

        x_in = sems("x_in", 2)
        tab_out, hl_out = sems("tab_out", 2), sems("hl_out", 2)
        tones, onehot_ready, prefix_ready, prefix_read = sem("tones"), sem("onehot_ready"), sem("prefix_ready"), sem("prefix_read")
        counted = sem("counted")
        place_ready, slot_ready, where_ready = sem("place_ready"), sem("slot_ready"), sem("where_ready")
        scattered = sems("scattered", 2)
        stats_ready, mv_ready, std_ready, rstd_ready, xn_ready = (
            sem("stats_ready"), sem("mv_ready"), sem("std_ready"), sem("rstd_ready"), sem("xn_ready"))
        var_ready, kstd_ready = sem("var_ready"), sem("kstd_ready")
        xt_ready, xt_copied = sem("xt_ready"), sem("xt_copied")
        h_ready, tab_ready = sem("h_ready"), sem("tab_ready")
        kv_ready, kv_copied = sem("kv_ready"), sem("kv_copied")
        kv_step, vs_ready, dt_done = sem("kv_step"), sem("vs_ready"), sem("dt_done")
        block = ctx.enter_context(nc.Block())
        b = g.bank
        RB, XB, HB, KB, VB, DB = (b[0], b[1]), b[2], b[3], b[4], b[5], b[6]

        @block.sync
        def _(sp):
            def step(j, first):
                for k in range(2):
                    i = 2 * j + k
                    if not first:
                        sp.wait_ge(xn_ready, i - 1)
                    sp.dma_start(xin[:, k, :], g.x[ds(i * TP, TP), :]).then_inc(x_in[k], 16)
                for k in range(2):
                    i = 2 * j + k
                    sp.wait_ge(tab_ready, i + 1)
                    sp.dma_start(g.table_d[ds(i * TP, TP), :], tab[:, k, :]).then_inc(tab_out[k], 16)
                    sp.dma_start(g.hl_d[ds(i * TP, TP), :], hlt[:, k, :]).then_inc(hl_out[k], 16)
            step(0, True)
            with sp.Fori(1, NT // 2) as j:
                step(j, False)
            for k in range(2):
                sp.wait_ge(tab_out[k], 16 * (NT // 2))
                sp.wait_ge(hl_out[k], 16 * (NT // 2))

        @block.gpsimd
        def _(pool):
            with pool.Fori(0, NT // 2) as j:
                for k in range(2):
                    after(pool, g, where_ready, 2 * (2 * j + k) + 2)
                    for c in range(EK):
                        pool.indirect_dma_start(g.sorted_d, bass.IndirectOffsetOnAxis(ap=where[:, k, c:c + 1], axis=0),
                                                load[:, k, c:c + 1], None).then_inc(scattered[k], 16)
            for k in range(2):
                pool.wait_ge(scattered[k], 16 * EK * (NT // 2))

        @block.vector
        def _(v):
            v.memset(tab[:, :, :], 1.0).then_inc(tones, 1)

            def normalise(i, k):
                v.wait_ge(std_ready, i + 1)
                v.reciprocal(rstd[:, :], std[:, :]).then_inc(rstd_ready, 1)
                if not (isinstance(i, int) and i < 2):
                    v.wait_ge(xt_ready, i - 1)
                v.wait_ge(rstd_ready, i + 1)
                v.tensor_scalar(xn[:, k, :], xin[:, k, :], mv[:, 0:1], rstd[:, 0:1], ALU.subtract, ALU.mult).then_inc(xn_ready, 1)

            def variances(i, k):
                v.wait_ge(kv_copied, 4 * i + 4)
                v.tensor_reduce(var[:, :], sq[:, k, :].rearrange("p (h f) -> p h f", f=MF), axis=AX.X, op=ALU.add).then_inc(var_ready, 1)

            def scale_values(i, k):
                v.wait_ge(kstd_ready, i + 1)
                v.reciprocal(kvr[:, :], kstd[:, :]).then_inc(kv_step, 1)
                v.wait_ge(kv_step, 2 * i + 1)
                v.tensor_tensor(scl[:, :], kvr[:, 0:MH], kvr[:, MH:2 * MH], ALU.mult).then_inc(kv_step, 1)
                v.wait_ge(kv_step, 2 * i + 2)
                v.tensor_tensor(vs[:, k, :].rearrange("p (h f) -> p h f", f=MF),
                                vc[:, k, :].rearrange("p (h f) -> p h f", f=MF),
                                bc(scl[:, :].unsqueeze(2), [TP, MH, MF]), ALU.mult).then_inc(vs_ready, 1)

            def step(j, first):
                for k in range(2):
                    i = 2 * j + k
                    if not (first and k == 0):
                        v.wait_ge(counted, 2 * i)
                    v.wait_ge(x_in[k], 16 * j + 16)
                    v.bn_stats(stats[:, :], xin[:, k, :]).then_inc(stats_ready, 1)
                    for s in range(2):
                        for c in range(S):
                            if s * S + c == EK - 1:
                                v.wait_ge(stats_ready, i + 1)
                            v.tensor_scalar(onehot[:, s, c, :], g.iotab[0:TP, :], g.bktf[:, ds(i * S + (s * HALF + c), 1)],
                                            None, ALU.is_equal).then_inc(onehot_ready, 1)
                    v.bn_aggr(mv[:, :], stats[:, :]).then_inc(mv_ready, 1)
                    for c in range(S):
                        if c == 1:
                            normalise(i, k)
                        if c == 4 and not (first and k == 0):
                            variances(i - 1, 1 - k)
                        if c == 6 and not (first and k == 0):
                            scale_values(i - 1, 1 - k)
                        for s in range(2):
                            n = c * 2 + s
                            v.wait_ge(prefix_ready, EK * i + (n + 1))
                            if not (first and k == 0 and n < 2):
                                v.wait_ge(prefix_read, EK * i + (n - 1))
                            v.scalar_tensor_tensor(junk[:, s, :], onehot[:, s, c, :], 1.0, RB[s][0:TP, 0:NB], ALU.mult, ALU.mult,
                                                   accum_out=place[:, n:n + 1]).then_inc(prefix_read, 1)
                    v.wait_ge(prefix_read, EK * i + EK)
                    v.tensor_copy(placei[:, :], place[:, :]).then_inc(place_ready, 1)
                    v.wait_ge(place_ready, i + 1)
                    v.tensor_scalar(slot[:, :], placei[:, :], 127, None, ALU.bitwise_and).then_inc(slot_ready, 1)
                    v.tensor_scalar(chunk[:, :], placei[:, :], 7, None, ALU.arith_shift_right).then_inc(slot_ready, 1)
                    v.wait_ge(slot_ready, 2 * i + 2)
                    if not first:
                        v.wait_ge(scattered[k], 16 * EK * j)
                    v.scalar_tensor_tensor(where[:, k, :], slot[:, :], float(NCH), chunk[:, :], ALU.mult, ALU.add).then_inc(where_ready, 1)
                    v.tensor_copy(load[:, k, :].rearrange("p (c s) -> p s c", s=2),
                                  g.packi[:, :].rearrange("p (s c) -> p s c", s=2)[:, :, ds(i * S, S)]).then_inc(where_ready, 1)
            step(0, True)
            with v.Fori(1, NT // 2) as j:
                step(j, False)
            variances(NT - 1, 1)
            scale_values(NT - 1, 1)

        @block.tensor
        def _(pe):
            for s in range(2):
                pe.matmul(RB[s][:, 0:NB], g.ones[0:1, :], g.firsts[0:1, s, :], start=True, stop=True)
            pe.matmul(DB[:, :], g.zero[:, 0:128], g.zero[:, :], start=True, stop=True)

            def product(i, k):
                pe.wait_ge(vs_ready, i + 1)
                for p in range(4):
                    m = pe.matmul(DB[:, p * 128:(p + 1) * 128], vs[:, k, p * 128:(p + 1) * 128], kc[:, k, p * 128:(p + 1) * 128],
                                  start=False, stop=True, skip_group_check=True)
                m.then_inc(dt_done, 1)

            def turn(i, k, first):
                pe.wait_ge(xn_ready, i + 1)
                if not first:
                    pe.wait_ge(xt_copied, 2 * i)
                for q in range(2):
                    m = pe.transpose(XB[:, q * 128:q * 128 + TP], xn[:, k, q * 128:(q + 1) * 128], g.ident[0:TP, 0:TP])
                m.then_inc(xt_ready, 1)

            def table(i, k, first):
                pe.wait_ge(xt_copied, 2 * i + 1)
                if not first:
                    pe.wait_ge(tab_ready, i)
                for q in range(2):
                    m = pe.matmul(HB[0:TP, 0:D + 2 * GH], xT[:, k, q, :], g.wa[:, q, :], start=(q == 0), stop=(q == 1))
                m.then_inc(h_ready, 1)

            def keys(i, k, first):
                if not first:
                    pe.wait_ge(kv_copied, 4 * i - 2)
                for q in range(2):
                    m = pe.matmul(KB[0:TP, :], xT[:, k, q, :], g.wkvT[:, q, 0:INNER], start=(q == 0), stop=(q == 1))
                m.then_inc(kv_ready, 1)

            def values(i, k, q, first):
                if q == 0 and not first:
                    pe.wait_ge(kv_copied, 4 * i)
                m = pe.matmul(VB[0:TP, :], xT[:, k, q, :], g.wkvT[:, q, INNER:2 * INNER], start=(q == 0), stop=(q == 1))
                if q == 1:
                    m.then_inc(kv_ready, 1)

            def step(j, first):
                for k in range(2):
                    i = 2 * j + k
                    start, second = first and k == 0, first and k == 1
                    for c in range(S + 1):
                        for s in range(2):
                            if c > 0:
                                pe.wait_ge(prefix_read, EK * i + (2 * c + s - 1))
                                m = pe.matmul(RB[s][0:TP, 0:NB], g.geb[0:TP, 0:TP], onehot[:, s, c - 1, :], start=False, stop=True, skip_group_check=True)
                                if c == S:
                                    m.then_inc(counted, 1)
                            if c < S:
                                pe.wait_ge(onehot_ready, EK * i + (s * S + c + 1))
                                pe.matmul(RB[s][0:TP, 0:NB], g.ltb[0:TP, 0:TP], onehot[:, s, c, :], start=False, stop=True, skip_group_check=True).then_inc(prefix_ready, 1)
                        if c < 2 and not start:
                            values(i - 1, 1 - k, c, second)
                        if c == 3:
                            turn(i, k, start)
                        if c == 5:
                            table(i, k, start)
                    if not start:
                        product(i - 1, 1 - k)
                    keys(i, k, start)
            step(0, True)
            with pe.Fori(1, NT // 2) as j:
                step(j, False)
            for q in range(2):
                values(NT - 1, 1, q, False)
            product(NT - 1, 1)

        @block.scalar
        def _(act):
            def keep(w, i, k, first):
                bk, kept, used = ((KB, kc, dt_done), (VB, vc, vs_ready))[w]
                act.wait_ge(kv_ready, 2 * i + (w + 1))
                if not (first or isinstance(i, int) and i < 2):
                    act.wait_ge(used, i - 1)
                act.copy(kept[:, k, :], bk[0:TP, :]).then_inc(kv_copied, 1)
                act.activation(sq[:, k, w * INNER:(w + 1) * INNER], bk[0:TP, :], ACT.Square).then_inc(kv_copied, 1)

            def heads(i):
                act.wait_ge(var_ready, i + 1)
                act.activation(kstd[:, :], var[:, :], ACT.Sqrt, bias=g.eps[0:TP, :], scale=1.0 / MF).then_inc(kstd_ready, 1)

            def step(j, first):
                for k in range(2):
                    i = 2 * j + k
                    act.wait_ge(mv_ready, i + 1)
                    act.activation(std[:, :], mv[:, 1:2], ACT.Sqrt, bias=g.eps[0:TP, :]).then_inc(std_ready, 1)
                    if not (first and k == 0):
                        keep(1, i - 1, 1 - k, first)
                    act.wait_ge(xt_ready, i + 1)
                    if not first:
                        act.wait_ge(kv_ready, 2 * i - 2)
                    xb = XB[:, 0:256].rearrange("p (q n) -> p q n", q=2)[:, :, 0:TP]
                    act.copy(xT[:, k, :, :], xb).then_inc(xt_copied, 1)
                    act.copy(g.xnT[:, ds(i, 1), :, :].rearrange("p a q n -> p (a q) n"), xb).then_inc(xt_copied, 1)
                    if not (first and k == 0):
                        heads(i - 1)
                    act.wait_ge(h_ready, i + 1)
                    if first and k == 0:
                        act.wait_ge(tones, 1)
                    if not first:
                        act.wait_ge(tab_out[k], 16 * j)
                        act.wait_ge(hl_out[k], 16 * j)
                    act.copy(tab[:, k, 0:TW].rearrange("p (h f) -> p h f", f=HW)[:, :, 0:GF],
                             HB[0:TP, 0:D].rearrange("p (h f) -> p h f", f=GF))
                    act.copy(tab[:, k, TW:ROW], HB[0:TP, D:D + GH])
                    act.copy(hlt[:, k, :], HB[0:TP, D + GH:D + 2 * GH]).then_inc(tab_ready, 1)
                    keep(0, i, k, first)
            step(0, True)
            step(1, False)
            with act.Fori(2, NT // 2) as j:
                step(j, False)
            keep(1, NT - 1, 1, False)
            heads(NT - 1)


def chunk_tables(nc, g):
    with ExitStack() as ctx:
        t = Parts(nc, ctx, "chunks")
        sb, sem = t.sb, t.sem
        packed = sb("packed", [128, NCH], I32)
        loci = sb("loci", [128, NCH], I32)
        fc, ec = sb("fc", [NBT, 2]), sb("ec", [NBT, 2])
        below, oh, starts = sb("below", [NBT, 2, NCH]), sb("oh", [NBT, 2, NCH]), sb("starts", [NBT, 2, NCH])
        hlb = sb("hlb", [NBT, 2, BR * GH])
        hlp = sb("hlp", [NBT, 2, GH, BR])
        base, nf, ni = sb("base", [NBT, 2]), sb("nf", [NBT, 2, BR]), sb("ni", [NBT, 2, BR], I32)
        dT, mixA = sb("dT", [128, 4, 128]), sb("mixA", [128, 4, D])
        list_in, cols_in, hl_in, n_out, n_in = sem("list_in"), sem("cols_in"), sem("hl_in"), sem("n_out"), sem("n_in")
        unpack, table, hlp_ready, oh_ready, st_ready = sem("unpack"), sem("table"), sem("hlp_ready"), sem("oh_ready"), sem("st_ready")
        n_step, n_ready, dz, dt_ready = sem("n_step"), sem("n_ready"), sem("dz"), sem("dt_ready")
        a_done, a_ready, p_done = sem("a_done"), sem("a_ready"), sem("p_done")
        rows_done = sem("rows_done")
        block = ctx.enter_context(nc.Block())
        b = g.bank
        H = NCH // 2

        @block.sync
        def _(sp):
            sp.dma_start(packed[:, :], g.sorted_d.rearrange("(p c) a -> p (c a)", p=128)).then_inc(list_in, 16)
            for s, dst in ((0, fc), (1, ec)):
                sp.dma_start(dst[:, :], g.cols_d[s, :].rearrange("(p t) -> p t", t=2)).then_inc(cols_in, 16)
            sp.dma_start(hlb[:, :, :], g.hl_d.rearrange("(p t r) h -> p t (r h)", t=2, r=BR)).then_inc(hl_in, 16)
            sp.wait_ge(n_ready, 1)
            sp.dma_start(g.node_d.rearrange("(p t r) a -> p t (r a)", t=2, r=BR), ni[:, :, :]).then_inc(n_out, 16)
            sp.wait_ge(n_out, 16)
            sp.dma_start(g.nodeidx[:, :], g.node_d[0:N, :].rearrange("(t p) a -> p (t a)", p=TP),
                         allow_slow_non_contiguous=True).then_inc(n_in, 16)
            sp.wait_ge(n_in, 16)

        @block.vector
        def _(v):
            v.wait_ge(list_in, 16)
            v.tensor_scalar(g.colidx[:, :], packed[:, :], (1 << COLBITS) - 1, None, ALU.bitwise_and)
            v.tensor_scalar(loci[:, :], packed[:, :], COLBITS, None, ALU.arith_shift_right).then_inc(unpack, 1)
            v.wait_ge(unpack, 1)
            v.tensor_copy(g.local[:, :], loci[:, :])
            v.wait_ge(hl_in, 16)
            v.tensor_copy(hlp[:, :, :, :], hlb[:, :, :].rearrange("p t (r h) -> p t h r", h=GH)).then_inc(hlp_ready, 1)
            v.wait_ge(cols_in, 32)
            io = g.iota[0:NBT, :]
            for s in range(2):
                v.tensor_scalar(below[:, s, :], io, ec[:, s:s + 1], None, ALU.is_lt).then_inc(table, 1)
                v.wait_ge(table, s + 1)
                v.scalar_tensor_tensor(oh[:, s, :], io, fc[:, s:s + 1], below[:, s, :], ALU.is_ge, ALU.mult).then_inc(oh_ready, 1)
                v.tensor_scalar(starts[:, s, :], io, fc[:, s:s + 1], -BIG, ALU.is_equal, ALU.mult).then_inc(st_ready, 1)
            v.tensor_scalar(base[:, :], ec[:, :], -1.0, float(BR), ALU.add, ALU.mult).then_inc(n_step, 1)
            v.wait_ge(n_step, 1)
            for s in range(2):
                v.tensor_scalar(nf[:, s, :], io[:, 0:BR], base[:, s:s + 1], None, ALU.add).then_inc(n_step, 1)
            v.wait_ge(n_step, 3)
            v.tensor_copy(ni[:, :, :], nf[:, :, :]).then_inc(n_ready, 1)
            v.memset(dT[:, :, :], 0.0).then_inc(dz, 1)
            v.wait_ge(dz, 1)
            for h in range(2):
                r = slice(64 * h, 64 * h + 64)
                v.tensor_copy(dT[r, :, r], b[6][r, :].rearrange("p (q c) -> p q c", q=4)[:, :, r]).then_inc(dt_ready, 1)
            v.wait_ge(rows_done, 4)
            for hf in range(2):
                v.tensor_copy(g.hlc[:, hf * H:(hf + 1) * H], b[hf][:, 0:H])
                v.tensor_copy(g.reset[:, hf * H:(hf + 1) * H], b[2 + hf][:, 0:H])
            for q in range(2):
                v.wait_ge(a_done, q + 1)
                v.tensor_copy(mixA[:, 2 * q:2 * q + 2, :], b[4 + q][:, :].rearrange("p (q c) -> p q c", q=2)).then_inc(a_ready, 1)
            v.wait_ge(p_done, 1)
            v.tensor_scalar(g.mixP[:, :, :], b[7][:, :].rearrange("p (q c) -> p q c", q=2), 1.0 / N, None, ALU.mult)

        @block.tensor
        def _(pe):
            pe.wait_ge(hlp_ready, 1)
            pe.wait_ge(oh_ready, 2)
            for hf in range(2):
                for s in range(2):
                    m = pe.matmul(b[hf][:, 0:H], hlp[:, s, :, :], oh[:, s, hf * H:(hf + 1) * H], start=(s == 0), stop=(s == 1))
                m.then_inc(rows_done, 1)
            pe.wait_ge(st_ready, 2)
            for hf in range(2):
                for s in range(2):
                    m = pe.matmul(b[2 + hf][:, 0:H], g.ones[0:NBT, :], starts[:, s, hf * H:(hf + 1) * H], start=(s == 0), stop=(s == 1))
                m.then_inc(rows_done, 1)
            pe.wait_ge(dt_ready, 2)
            for q in range(4):
                m = pe.matmul(b[4 + q // 2][:, (q % 2) * D:(q % 2 + 1) * D], dT[:, q, :], g.woT[:, q, :], start=True, stop=True)
                if q % 2:
                    m.then_inc(a_done, 1)
            pe.wait_ge(a_ready, 2)
            for k in range(2):
                for q in range(4):
                    m = pe.matmul(b[7][:, k * D:(k + 1) * D], g.wq[:, q, k * 128:(k + 1) * 128], mixA[:, q, :],
                                  start=(q == 0), stop=(q == 3))
            m.then_inc(p_done, 1)


def edge_loop(nc, g):
    with ExitStack() as ctx:
        t = Parts(nc, ctx, "edge")
        sb, sem, sems = t.sb, t.sem, t.sems
        gat = sb("gat", [128, RING, GU, ROW])
        idx = sb("idx", [128, 2, RING * GU // 2], I32)
        mask = sb("mask", [128, 2, GU, BR])
        scr = sb("scr", [128, 2, GU, GH, BR])
        mch = sb("mch", [128, 2, GU])
        mrun, srun = sb("mrun", [128, 2, GU]), sb("srun", [128, 1 + NCH])
        zrun = sb("zrun", [128, GU])
        bias1, bias2 = sb("bias1", [128, 2, GU]), sb("bias2", [128, 2, GU])
        dif, dif2, fac = sb("dif", [128, GU]), sb("dif2", [128, 3, GU]), sb("fac", [128, 3, GU])
        hl2 = sb("hl2", [128, NCH])
        e1, e2 = sb("e1", [128, 2, GU * 128]), sb("e2", [128, 2, GU * 128])
        wt = sb("wt", [128, 2, GU * 128])
        wts = sb("wts", [128, 2, GU * 128])
        acc = sb("acc", [128, 3, GU, HW])

        gathered = sems("gathered", RING)
        idx_ready = sem("idx_ready")
        init = sem("init")
        mask_ready, scr_ready, scr_used = sem("mask_ready"), sem("scr_ready"), sem("scr_used")
        mch_ready, mrun_ready, zrun_ready, srun_ready = sem("mch_ready"), sem("mrun_ready"), sem("zrun_ready"), sem("srun_ready")
        bias_ready, dif_ready, dif2_ready = sem("bias_ready"), sem("dif_ready"), sem("dif2_ready")
        exp_ready, fac_ready, wt_ready, wtt_ready, wts_ready = sem("exp_ready"), sem("fac_ready"), sem("wt_ready"), sem("wtt_ready"), sem("wts_ready")
        agg_ready, acc_ready = sem("agg_ready"), sem("acc_ready")
        sums_out = sems("sums_out", 3)
        block = ctx.enter_context(nc.Block())
        ST, WB, AB = g.bank[0:2], g.bank[2:4], g.bank[4:6]

        def groups(eng, step):
            for u in range(RING):
                step(u, u, 0, False)
            with eng.Fori(1, NG // RING) as m:
                for u in range(RING):
                    step(m * RING + u, u, m, True)

        @block.gpsimd
        def _(pool):
            hf = RING * GU // 2

            def indices(half, c0, n, first):
                if not first:
                    for u in range(3 * half, 3 * half + 3):
                        pool.wait_ge(gathered[u], 16 * GU * n)
                pool.tensor_copy(idx[:, half, :], g.colidx[:, ds(c0, hf)]).then_inc(idx_ready, 1)

            def body(m, first):
                for half in range(2):
                    indices(half, m * (2 * hf) + half * hf, m, first)
                    after(pool, g, idx_ready, 2 * m + (half + 1))
                    for u in range(3 * half, 3 * half + 3):
                        if not first:
                            after(pool, g, agg_ready, m * RING + (u - RING + 1))
                        for c in range(GU):
                            pool.indirect_dma_start(gat[:, u, c, :], None, g.table_d,
                                                    bass.IndirectOffsetOnAxis(ap=idx[:, half, (u % 3) * GU + c:(u % 3) * GU + c + 1], axis=0)
                                                    ).then_inc(gathered[u], 16)
            body(0, True)
            with pool.Fori(1, NG // RING) as m:
                body(m, False)

        @block.vector
        def _(v):
            v.tensor_scalar(hl2[:, :], g.hlc[:, :], SLOPE, None, ALU.mult)
            v.memset(mrun[:, 1, :], -BIG)
            v.memset(srun[:, 0:1], -BIG)
            v.memset(acc[:, 2, :, :], 0.0).then_inc(init, 1)
            v.wait_ge(init, 1)

            def A1(n, u, m, late):
                k = u % 2
                v.tensor_tensor(mask[:, k, :, :], bc(g.iota[:, 0:BR].unsqueeze(1), [128, GU, BR]),
                                bc(g.local[:, ds(n * GU, GU)].unsqueeze(2), [128, GU, BR]), ALU.not_equal).then_inc(mask_ready, 1)

            def A2(n, u, m, half):
                k = u % 2
                if half == 0:
                    v.wait_ge(gathered[u], 16 * GU * (m + 1))
                    v.wait_ge(mask_ready, n + 1)
                for c in (2 * half, 2 * half + 1):
                    i = v.scalar_tensor_tensor(scr[:, k, c, :, :], bc(mask[:, k, c, :].unsqueeze(1), [128, GH, BR]), -BIG,
                                               bc(gat[:, u, c, TW:ROW].unsqueeze(2), [128, GH, BR]), ALU.mult, ALU.add)
                i.then_inc(scr_ready, 1)

            def chain(n, u, k):
                o, t3 = 1 - k, u % 3
                hl = g.hlc[:, ds(n * GU, GU)]
                cols, later = ds(n * GU, GU), ds(n * GU + 1, GU)

                def b1():
                    v.wait_ge(scr_used, n + 1)
                    v.tensor_reduce(mch[:, k, :], ST[k][:, :].rearrange("p (c e) -> p c e", c=GU), axis=AX.X, op=ALU.max).then_inc(mch_ready, 1)

                def b2():
                    v.wait_ge(mch_ready, n + 1)
                    v.tensor_tensor_scan(mrun[:, k, :], g.reset[:, cols], mch[:, k, :], mrun[:, o, GU - 1:GU], ALU.add, ALU.max).then_inc(mrun_ready, 1)

                def b3():
                    v.wait_ge(mrun_ready, n + 1)
                    v.scalar_tensor_tensor(zrun[:, :], mrun[:, k, :], -FLOOR, hl, ALU.max, ALU.add).then_inc(zrun_ready, 1)

                def b4():
                    v.wait_ge(zrun_ready, n + 1)
                    v.scalar_tensor_tensor(srun[:, later], zrun[:, :], SLOPE, zrun[:, :], ALU.mult, ALU.max).then_inc(srun_ready, 1)

                def b5():
                    v.wait_ge(srun_ready, n + 1)
                    v.tensor_tensor(bias1[:, k, :], hl, srun[:, later], ALU.subtract)
                    v.tensor_tensor(bias2[:, k, :], hl2[:, cols], srun[:, later], ALU.subtract).then_inc(bias_ready, 1)
                    v.tensor_tensor(dif[:, :], srun[:, cols], srun[:, later], ALU.subtract).then_inc(dif_ready, 1)

                def b6():
                    v.wait_ge(dif_ready, n + 1)
                    v.tensor_tensor(dif2[:, t3, :], dif[:, :], g.reset[:, cols], ALU.add).then_inc(dif2_ready, 1)
                return [b1, b2, b3, b4, b5, b6]

            def C1(n, k):
                v.wait_ge(exp_ready, n + 1)
                v.tensor_tensor(wt[:, k, :], e1[:, k, :], e2[:, k, :], ALU.max).then_inc(wt_ready, 1)

            def sums(n, u, sent):
                k, r, o = u % 2, u % 3, (u - 1) % 3

                def d(c):
                    def f():
                        if c == 0:
                            v.wait_ge(agg_ready, n + 1)
                        before = acc[:, r, c - 1, :] if c else acc[:, o, GU - 1, :]
                        if not (isinstance(n, int) and n == 0 and c == 0):
                            v.wait_ge(acc_ready, n * GU + c)
                        if c == 0 and not (isinstance(n, int) and n < 3):
                            v.wait_ge(sums_out[r], 64 * sent)
                        v.scalar_tensor_tensor(acc[:, r, c, :], before, fac[:, r, c:c + 1], AB[k][:, c * HW:(c + 1) * HW],
                                               ALU.mult, ALU.add).then_inc(acc_ready, 1)
                    return f
                return [d(c) for c in range(GU)]

            def step(n, u, m, late):
                real = (lambda q: late or n >= q)
                b = chain(n - 1, (u - 1) % RING, (u - 1) % 2) if real(1) else [lambda: None] * 6
                if real(4):
                    d = sums(n - 4, (u - 4) % RING, 2 * m + (u - 4) // 3)
                else:
                    d = [lambda: None] * GU
                b[0]()
                d[0]()
                b[1]()
                d[1]()
                b[2]()
                d[2]()
                b[3]()
                A1(n, u, m, late)
                b[4]()
                A2(n, u, m, 0)
                b[5]()
                A2(n, u, m, 1)
                d[3]()
                if real(2):
                    C1(n - 2, u % 2)
            groups(v, step)
            for n in range(NG, NG + 4):
                u = n % RING
                if n == NG:
                    for f in chain(n - 1, (u - 1) % RING, (u - 1) % 2):
                        f()
                for f in sums(n - 4, (u - 4) % RING, (n - 4) // 3):
                    f()
                if n <= NG + 1:
                    C1(n - 2, u % 2)

        @block.tensor
        def _(pe):
            def scores(n, u):
                k = u % 2
                if not (isinstance(n, int) and n < 2):
                    pe.wait_ge(exp_ready, n - 1)
                for c in range(GU):
                    if c % 2 == 0:
                        pe.wait_ge(scr_ready, 2 * n + c // 2 + 1)
                    m = pe.transpose(ST[k][:, c * 128:(c + 1) * 128], scr[:, k, c, :, :].rearrange("p h r -> p (h r)"), g.ident)
                m.then_inc(scr_used, 1)

            def weights(n, u):
                k = u % 2
                pe.wait_ge(wt_ready, n + 1)
                if not (isinstance(n, int) and n < 2):
                    pe.wait_ge(wts_ready, n - 1)
                for c in range(GU):
                    m = pe.transpose(WB[k][:, c * 128:(c + 1) * 128], wt[:, k, c * 128:(c + 1) * 128], g.ident)
                m.then_inc(wtt_ready, 1)

            def aggregate(n, u):
                k = u % 2
                pe.wait_ge(wts_ready, n + 1)
                if not (isinstance(n, int) and n < 2):
                    pe.wait_ge(acc_ready, GU * (n - 1))
                for c in range(GU):
                    for h in range(GH):
                        m = pe.matmul(AB[k][h * BR:(h + 1) * BR, c * HW:(c + 1) * HW],
                                      wts[:, k, c * 128 + h * BR:c * 128 + (h + 1) * BR], gat[:, u, c, h * HW:(h + 1) * HW],
                                      start=True, stop=True)
                m.then_inc(agg_ready, 1)

            def step(n, u, m, late):
                scores(n, u)
                if late or n >= 2:
                    weights(n - 2, (u - 2) % RING)
                    aggregate(n - 2, (u - 2) % RING)
            groups(pe, step)
            for n in range(NG - 2, NG):
                weights(n, n % RING)
                aggregate(n, n % RING)

        @block.scalar
        def _(act):
            def exps(n, u):
                k = u % 2
                act.wait_ge(bias_ready, n + 1)
                if not (isinstance(n, int) and n < 2):
                    act.wait_ge(wt_ready, n - 1)
                for c in range(GU):
                    s = slice(c * 128, (c + 1) * 128)
                    act.activation(e1[:, k, s], ST[k][:, s], ACT.Exp, bias=bias1[:, k, c:c + 1])
                    i = act.activation(e2[:, k, s], ST[k][:, s], ACT.Exp, bias=bias2[:, k, c:c + 1], scale=SLOPE)
                i.then_inc(exp_ready, 1)
                act.wait_ge(dif2_ready, n + 1)
                if not (isinstance(n, int) and n < 3):
                    act.wait_ge(acc_ready, GU * (n - 2))
                act.activation(fac[:, u % 3, :], dif2[:, u % 3, :], ACT.Exp).then_inc(fac_ready, 1)

            def copy(n, u):
                k = u % 2
                act.wait_ge(wtt_ready, n + 1)
                if not (isinstance(n, int) and n < 2):
                    act.wait_ge(agg_ready, n - 1)
                act.copy(wts[:, k, :], WB[k][:, :]).then_inc(wts_ready, 1)

            def step(n, u, m, late):
                if late or n >= 1:
                    exps(n - 1, (u - 1) % RING)
                if late or n >= 2:
                    copy(n - 2, (u - 2) % RING)
            groups(act, step)
            exps(NG - 1, (NG - 1) % RING)
            copy(NG - 2, (NG - 2) % RING)
            copy(NG - 1, (NG - 1) % RING)

        @block.sync
        def _(sp):
            out = g.sums_d.rearrange("(c r) (h f) -> h r c f", r=BR, h=GH)

            def step(n, u, m, late):
                sp.wait_ge(acc_ready, GU * (n + 1))
                for h in range(GH):
                    sp.dma_start(out[h][:, ds(n * GU, GU), :], acc[h * BR:(h + 1) * BR, u % 3, :, :]).then_inc(sums_out[u % 3], 16)
            groups(sp, step)
            for r in range(3):
                sp.wait_ge(sums_out[r], 64 * (NG // 3))


def token_loop(nc, g):
    with ExitStack() as ctx:
        t = Parts(nc, ctx, "token")
        sb, sem, sems = t.sb, t.sem, t.sems
        idx = sb("tidx", [TP, 2, TB], I32)
        sums = sb("sums", [TP, 2, TB, TW])
        xin = sb("txin", [TP, 2, TB, D])
        x2 = sb("x2", [TP, 2, TB, D])
        xf = sb("xf", [TP, 2, TB, XW])
        token, w1 = sb("token", [TP, NT]), sb("w1", [TP, TB])
        xTs = sb("xTs", [128, 2, 2, TP])
        den, rden = sb("den", [TP, TB, GH]), sb("rden", [TP, TB, GH])
        stats, mv = sb("tstats", [TP, TB, 6]), sb("tmv", [TP, TB, 2])
        var2, std2, r12 = sb("var2", [TP, TB]), sb("std2", [TP, TB]), sb("r12", [TP, TB])
        gbc, bbc, boutbc, brbc = sb("gbc", [TP, D]), sb("bbc", [TP, D]), sb("boutbc", [TP, D]), sb("brbc", [TP, NE])
        xfT = sb("xfT", [128, 2, 2, TP])
        lg = sb("lg", [TP, TB, NE])
        top, topi, topf = sb("top", [TP, TB, NE]), sb("topi", [TP, TB, NE], U32), sb("topf", [TP, TB, NE])
        one1, one2 = sb("one1", [TP, TB, NE]), sb("one2", [TP, TB, NE])
        both = sb("both", [TP, TB, NE], BF16)
        base, ranks = sb("base", [TP, NE]), sb("ranks", [TP, TB, NE])
        pj = sb("pj", [TP, 2, TB, NE])
        pos = sb("pos", [TP, 2, TB])
        posi = sb("posi", [TP, 2, 2, TB], I32)
        dl, el, el1 = sb("dl", [TP, TB]), sb("el", [TP, TB]), sb("el1", [TP, TB])
        onesb = sb("onesb", [TP, 128], BF16)
        ebase = sb("ebase", [128, NE])
        cnts, cnti, cntj, nch = sb("cnts", [128, NE]), sb("cnti", [128, NE], I32), sb("cntj", [128, NE], I32), sb("nch", [128, NE])
        ends, begin, last = sb("ends", [128, NE]), sb("begin", [128, NE]), sb("last", [128, 1])
        prow, pcol = sb("prow", [128, 1]), sb("pcol", [128, 1])
        padi = sb("padi", [128, NE], I32)
        zrow = sb("zrow", [128, XW])
        chc, past, pastn = sb("chc", [128, MC]), sb("past", [128, NE - 1, MC]), sb("pastn", [128, NE - 1, MC])
        ex, bg, df, rw = g.expert_of, sb("bg", [128, MC]), sb("df", [128, MC]), sb("rw", [128, MC])

        gb_in = sem("gb_in")
        x_in, sums_in = sems("tx_in", 2), sems("sums_in", 2)
        x2_out, sent = sems("x2_out", 2), sems("sent", 2)
        idx_ready = sem("tidx_ready")
        xts_ready, mix_ready, mix_read = sem("xts_ready"), sem("mix_ready"), sem("mix_read")
        front_step, back_step, end_step = sem("front_step"), sem("back_step"), sem("end_step")
        sums_used, x2_ready, xf_ready, pos_ready = sem("sums_used"), sem("x2_ready"), sem("xf_ready"), sem("pos_ready")
        xft_ready, xft_copied, lg_ready, lg_read = sem("xft_ready"), sem("xft_copied"), sem("lg_ready"), sem("lg_read")
        var2_ready, std2_ready = sem("var2_ready"), sem("std2_ready")
        diff_ready, el_ready = sem("diff_ready"), sem("el_ready")
        both_ready, rank_ready, rank_read, total_ready = sem("both_ready"), sem("rank_ready"), sem("rank_read"), sem("total_ready")
        pad_step = sem("pad_step")
        base_read, ebase_ready, pad_ready, pad_out = sem("base_read"), sem("ebase_ready"), sem("pad_ready"), sem("pad_out")
        block = ctx.enter_context(nc.Block())
        b = g.bank
        MB, XB, LB, PB, RB = (b[0], b[1], b[7]), b[2:4], b[4], b[5], b[6]
        stored = [min(c // 2 * 2 + 2, TB) for c in range(TB)]

        def mixed(c):
            return MB[c // 2][0:TP, (c % 2) * D:(c % 2 + 1) * D]

        def view(ap, m):
            return ap[ds(m * (TB * TP), TB * TP), :].rearrange("(t p) f -> p t f", p=TP)

        @block.sync
        def _(sp):
            sp.dma_start(gbc[:, :], g.gamma.partition_broadcast(TP)).then_inc(gb_in, 16)
            sp.dma_start(bbc[:, :], g.beta.partition_broadcast(TP)).then_inc(gb_in, 16)
            sp.dma_start(boutbc[:, :], g.bout.partition_broadcast(TP)).then_inc(gb_in, 16)
            sp.dma_start(brbc[:, :], g.br.partition_broadcast(TP)).then_inc(gb_in, 16)

            def step(j, first):
                for k in range(2):
                    m = 2 * j + k
                    if not first:
                        sp.wait_ge(sums_used, 2 * m - 2)
                    sp.dma_start(xin[:, k, :, :], view(g.x, m)).then_inc(x_in[k], 16)
                for k in range(2):
                    m = 2 * j + k
                    sp.wait_ge(x2_ready, m + 1)
                    sp.dma_start(view(g.x2_d, m), x2[:, k, :, :]).then_inc(x2_out[k], 16)
            step(0, True)
            with sp.Fori(1, NBL // 2) as j:
                step(j, False)
            for k in range(2):
                sp.wait_ge(x2_out[k], 16 * (NBL // 2))

        @block.gpsimd
        def _(pool):
            def fetch(m, j, k, first):
                if not first:
                    pool.wait_ge(sums_in[k], 16 * TB * j)
                pool.tensor_copy(idx[:, k, :], g.nodeidx[:, ds(m * TB, TB)]).then_inc(idx_ready, 1)
                if not first:
                    pool.wait_ge(sums_used, 2 * m - 2)
                after(pool, g, idx_ready, m + 1)
                for c in range(TB):
                    pool.indirect_dma_start(sums[:, k, c, :], None, g.sums_d,
                                            bass.IndirectOffsetOnAxis(ap=idx[:, k, c:c + 1], axis=0)).then_inc(sums_in[k], 16)

            def send(m, k):
                after(pool, g, pos_ready, m + 1)
                for s in range(2):
                    for c in range(TB):
                        pool.indirect_dma_start(g.xs_d, bass.IndirectOffsetOnAxis(ap=posi[:, k, s, c:c + 1], axis=0),
                                                xf[:, k, c, :], None).then_inc(sent[k], 16)

            fetch(0, 0, 0, True)
            fetch(1, 0, 1, True)
            with pool.Fori(1, NBL // 2) as j:
                for k in range(2):
                    fetch(2 * j + k, j, k, False)
                    send(2 * j + (k - 2), k)
            for k in range(2):
                send(NBL - 2 + k, k)
            pool.wait_ge(pad_ready, 1)
            for e in range(NE):
                pool.indirect_dma_start(g.xs_d, bass.IndirectOffsetOnAxis(ap=padi[:, e:e + 1], axis=0), zrow[:, :], None).then_inc(pad_out, 16)
            for k in range(2):
                pool.wait_ge(sent[k], 32 * TB * (NBL // 2))
            pool.wait_ge(pad_out, 16 * NE)

        @block.scalar
        def _(act):
            def features(m, k, tiles, first):
                for c in tiles:
                    i = m * TB + c
                    r = (k * TB + c) % 2
                    if not (first and c < 2):
                        act.wait_ge(mix_ready, i - 1)
                    act.copy(xTs[:, r, :, :], g.xnT[:, ds(i, 1), :, :].rearrange("p a q n -> p (a q) n")).then_inc(xts_ready, 1)

            def turned(m, k):
                for c in range(TB):
                    i = m * TB + c
                    r = (k * TB + c) % 2
                    act.wait_ge(xft_ready, i + 1)
                    act.copy(xfT[:, r, :, :], XB[r][:, 0:256].rearrange("p (q n) -> p q n", q=2)[:, :, 0:TP]).then_inc(xft_copied, 1)

            def deviation(m):
                act.wait_ge(var2_ready, m + 1)
                act.activation(std2[:, :], var2[:, :], ACT.Sqrt).then_inc(std2_ready, 1)

            def exponential(m):
                act.wait_ge(diff_ready, m + 1)
                act.activation(el[:, :], dl[:, :], ACT.Exp).then_inc(el_ready, 1)

            def step(m, k):
                turned(m - 1, 1 - k)
                more = not (isinstance(m, int) and m == NBL - 1)
                if more:
                    features(m + 1, 1 - k, range(2), False)
                deviation(m)
                exponential(m - 1)
                if more:
                    features(m + 1, 1 - k, range(2, TB), False)
            features(0, 0, range(TB), True)
            features(1, 1, range(2), False)
            deviation(0)
            features(1, 1, range(2, TB), False)
            step(1, 1)
            with act.Fori(1, NBL // 2 - 1) as j:
                for k in range(2):
                    step(2 * j + k, k)
            for k in range(2):
                step(NBL - 2 + k, k)
            turned(NBL - 1, 1)
            exponential(NBL - 1)

        @block.tensor
        def _(pe):
            pe.wait_ge(ebase_ready, 1)
            pe.matmul(RB[:, 0:NE], g.ones[0:1, :], ebase[0:1, :], start=True, stop=True).then_inc(total_ready, 1)

            def front(m, k, first):
                for c in range(TB):
                    i = m * TB + c
                    r = (k * TB + c) % 2
                    pe.wait_ge(xts_ready, i + 1)
                    if not first:
                        pe.wait_ge(mix_read, (m - 1) * TB + stored[c])
                    pe.matmul(mixed(c), xTs[:, r, 0, :], g.mixP[:, 0, :], start=True, stop=False)
                    pe.matmul(mixed(c), xTs[:, r, 1, :], g.mixP[:, 1, :], start=False, stop=True).then_inc(mix_ready, 1)

            def logits(m, k, first):
                pe.wait_ge(xf_ready, m + 1)
                if not first:
                    pe.wait_ge(lg_read, m)
                for c in range(TB + 1):
                    i = m * TB + c
                    if c < TB:
                        r = (k * TB + c) % 2
                        if not (first and c < 2):
                            pe.wait_ge(xft_copied, i - 1)
                        for q in range(2):
                            u = pe.transpose(XB[r][:, q * 128:q * 128 + TP], xf[:, k, c, q * 128:(q + 1) * 128], g.ident[0:TP, 0:TP])
                        u.then_inc(xft_ready, 1)
                    if c > 0:
                        r = (k * TB + c - 1) % 2
                        pe.wait_ge(xft_copied, i)
                        o = LB[0:TP, (c - 1) * NE:c * NE]
                        pe.matmul(o, xfT[:, r, 0, :], g.wrs[:, 0, :], start=True, stop=False)
                        u = pe.matmul(o, xfT[:, r, 1, :], g.wrs[:, 1, :], start=False, stop=True)
                        u.then_inc(lg_ready, 1)

            def places(m, first):
                pe.wait_ge(both_ready, m + 1)
                if not first:
                    pe.wait_ge(rank_read, m)
                pe.matmul(PB[0:TP, 0:TB * NE], g.ltb[0:TP, 0:TP], both[:, :, :], start=True, stop=False)
                for c in range(TB - 1):
                    u = pe.matmul(PB[0:TP, (c + 1) * NE:TB * NE], onesb[:, 0:TP],
                                  bc(both[:, c, :].unsqueeze(1), [TP, TB - 1 - c, NE]), start=False, stop=(c == TB - 2))
                u.then_inc(rank_ready, 1)
                pe.wait_ge(base_read, m + 1)
                for c in range(TB):
                    u = pe.matmul(RB[:, 0:NE], onesb[:, :], both[:, c, :], start=False, stop=True, skip_group_check=True)
                u.then_inc(total_ready, 1)

            def step(m, k, first):
                logits(m - 1, 1 - k, first)
                if not (isinstance(m, int) and m == NBL - 1):
                    front(m + 1, 1 - k, False)
                places(m - 1, first)
            front(0, 0, True)
            front(1, 1, False)
            step(1, 1, True)
            with pe.Fori(1, NBL // 2 - 1) as j:
                for k in range(2):
                    step(2 * j + k, k, False)
            for k in range(2):
                step(NBL - 2 + k, k, False)
            logits(NBL - 1, 1, False)
            places(NBL - 1, False)

        @block.vector
        def _(v):
            v.memset(onesb[:, :], 1.0)
            v.tensor_scalar(ebase[:, :], g.iota[:, 0:NE], float(CAP), None, ALU.mult).then_inc(ebase_ready, 1)
            v.wait_ge(gb_in, 64)
            v.tensor_reduce(prow[:, :], g.cst[:, C_LT:C_LT + 128], axis=AX.X, op=ALU.add).then_inc(pad_step, 1)
            v.wait_ge(pad_step, 1)
            v.tensor_scalar(pcol[:, :], prow[:, :], -1.0, 127.0, ALU.mult, ALU.add)
            v.memset(zrow[:, :], 0.0)
            v.memset(xf[:, :, :, C_MN], float(-N)).then_inc(pad_step, 1)
            v.wait_ge(pad_step, 2)
            v.memset(zrow[:, C_E1:XW], -1.0)
            v.tensor_scalar(zrow[:, C_B:C_B + 1], pcol[:, :], float(2 * N), None, ALU.add)
            v.tensor_scalar(token[:, :], g.iota[0:TP, 0:NT], float(TP), pcol[0:TP, 0:1], ALU.mult, ALU.add).then_inc(pad_step, 1)
            v.wait_ge(pad_step, 3)
            FL, BL = 6, 9

            def chain(sem, m, per_block, n):
                count = [n]

                def link(ins):
                    count[0] += 1
                    ins.then_inc(sem, 1)
                    v.wait_ge(sem, m * per_block + count[0])
                return link

            def residual(m, j, k, first):
                link = chain(front_step, m, FL, 0)
                v.wait_ge(x_in[k], 16 * (j + 1))
                link(v.tensor_tensor(xin[:, k, :, :], xin[:, k, :, :], bc(boutbc[:, :].unsqueeze(1), [TP, TB, D]), ALU.add))
                v.wait_ge(sums_in[k], 16 * TB * (j + 1))
                s4 = sums[:, k, :, :].rearrange("p t (h f) -> p t h f", f=HW)
                link(v.tensor_scalar(den[:, :, :], s4[:, :, :, GF], 1e-16, None, ALU.max))
                link(v.reciprocal(rden[:, :, :], den[:, :, :]))
                if not first:
                    v.wait_ge(x2_out[k], 16 * j)
                th = x2[:, k, :, :].rearrange("p t (h f) -> p (t h) f", h=GH)
                ins = v.tensor_tensor(th, sums[:, k, :, :].rearrange("p t (h f) -> p (t h) f", f=HW)[:, :, 0:GF],
                                      bc(rden[:, :, :].rearrange("p t h -> p (t h)").unsqueeze(2), [TP, TB * GH, GF]), ALU.mult)
                ins.then_inc(sums_used, 1)
                v.wait_ge(sums_used, 2 * m + 1)
                v.tensor_tensor(x2[:, k, :, :], x2[:, k, :, :], xin[:, k, :, :], ALU.add).then_inc(sums_used, 1)
                v.wait_ge(sums_used, 2 * m + 2)
                for c in range(TB):
                    i = m * TB + c
                    v.wait_ge(mix_ready, m * TB + stored[c])
                    v.tensor_tensor(x2[:, k, c, :], x2[:, k, c, :], mixed(c), ALU.add).then_inc(mix_read, 1)
                for c in range(TB):
                    v.wait_ge(mix_read, m * TB + (c + 1))
                    ins = v.bn_stats(stats[:, c, :], x2[:, k, c, :])
                ins.then_inc(x2_ready, 1)
                after(v, g, x2_ready, m + 1)
                for c in range(TB):
                    ins = v.bn_aggr(mv[:, c, :], stats[:, c, :])
                link(ins)
                v.tensor_scalar(var2[:, :], mv[:, :, 1], 1.0 + EPS, EPS * EPS, ALU.mult, ALU.add).then_inc(var2_ready, 1)

            def normalise(m, j, k, first):
                link = chain(front_step, m, FL, 4)
                if not first:
                    v.wait_ge(sent[k], 32 * TB * j)
                    v.wait_ge(xft_ready, (m - 1) * TB)
                for c in range(TB):
                    ins = v.scalar_tensor_tensor(xf[:, k, c, 0:D], x2[:, k, c, :], mv[:, c, 0:1], gbc[:, :], ALU.subtract, ALU.mult)
                link(ins)
                v.wait_ge(std2_ready, m + 1)
                link(v.reciprocal(r12[:, :], std2[:, :]))
                for c in range(TB):
                    ins = v.scalar_tensor_tensor(xf[:, k, c, 0:D], xf[:, k, c, 0:D], r12[:, c:c + 1], bbc[:, :], ALU.mult, ALU.add)
                ins.then_inc(xf_ready, 1)

            def choose(m):
                link = chain(back_step, m, BL, 0)
                tiles = ds(m * TB, TB)
                v.wait_ge(lg_ready, (m + 1) * TB)
                v.tensor_tensor(lg[:, :, :], LB[0:TP, 0:TB * NE].rearrange("p (t e) -> p t e", e=NE),
                                bc(brbc[:, :].unsqueeze(1), [TP, TB, NE]), ALU.add).then_inc(lg_read, 1)
                v.wait_ge(total_ready, m + 1)
                v.wait_ge(lg_read, m + 1)
                v.tensor_copy(base[:, :], RB[0:TP, 0:NE]).then_inc(base_read, 1)
                for c in range(TB):
                    ins = v.max(top[:, c, :], lg[:, c, :])
                link(ins)
                v.tensor_tensor(dl[:, :], top[:, :, 1], top[:, :, 0], ALU.subtract).then_inc(diff_ready, 1)
                for c in range(TB):
                    ins = v.max_index(topi[:, c, :], top[:, c, :], lg[:, c, :])
                link(ins)
                link(v.tensor_copy(topf[:, :, :], topi[:, :, :]))
                io = bc(g.iota[0:TP, 0:NE].unsqueeze(1), [TP, TB, NE])
                v.tensor_tensor(one1[:, :, :], io, bc(topf[:, :, 0:1], [TP, TB, NE]), ALU.is_equal)
                link(v.tensor_tensor(one2[:, :, :], io, bc(topf[:, :, 1:2], [TP, TB, NE]), ALU.is_equal))
                v.tensor_tensor(both[:, :, :], one1[:, :, :], one2[:, :, :], ALU.add).then_inc(both_ready, 1)

            def route(m, k):
                link = chain(back_step, m, BL, 4)
                tiles = ds(m * TB, TB)
                v.wait_ge(el_ready, m + 1)
                link(v.tensor_scalar(el1[:, :], el[:, :], 1.0, None, ALU.add))
                link(v.reciprocal(w1[:, :], el1[:, :]))
                v.tensor_scalar(xf[:, k, :, C_B], token[:, tiles], float(N), None, ALU.add)
                v.tensor_copy(xf[:, k, :, C_E1], topf[:, :, 0])
                link(v.tensor_tensor(xf[:, k, :, C_W2], el[:, :], w1[:, :], ALU.mult))
                v.tensor_tensor(xf[:, k, :, C_DW], w1[:, :], xf[:, k, :, C_W2], ALU.subtract)
                v.wait_ge(rank_ready, m + 1)
                v.tensor_tensor(ranks[:, :, :], PB[0:TP, 0:TB * NE].rearrange("p (t e) -> p t e", e=NE),
                                bc(base[:, :].unsqueeze(1), [TP, TB, NE]), ALU.add).then_inc(rank_read, 1)
                v.wait_ge(rank_read, m + 1)
                v.tensor_tensor(pj[:, 0, :, :], ranks[:, :, :], one1[:, :, :], ALU.mult)
                link(v.tensor_tensor(pj[:, 1, :, :], ranks[:, :, :], one2[:, :, :], ALU.mult))
                link(v.tensor_reduce(pos[:, :, :], pj[:, :, :, :], axis=AX.X, op=ALU.add))
                v.tensor_copy(posi[:, k, :, :], pos[:, :, :]).then_inc(pos_ready, 1)

            def step(m, j, k, first):
                residual(m, j, k, first)
                choose(m - 1)
                normalise(m, j, k, first)
                route(m - 1, 1 - k)
            residual(0, 0, 0, True)
            normalise(0, 0, 0, True)
            step(1, 0, 1, True)
            with v.Fori(1, NBL // 2) as j:
                for k in range(2):
                    step(2 * j + k, j, k, False)
            choose(NBL - 1)
            route(NBL - 1, 1)

            e = [0]

            def link(ins):
                e[0] += 1
                ins.then_inc(end_step, 1)
                v.wait_ge(end_step, e[0])
            v.wait_ge(total_ready, NBL + 1)
            v.wait_ge(ebase_ready, 1)
            v.tensor_scalar(padi[:, :], RB[:, 0:NE], pcol[:, 0:1], None, ALU.add).then_inc(pad_ready, 1)
            link(v.tensor_tensor(cnts[:, :], RB[:, 0:NE], ebase[:, :], ALU.subtract))
            link(v.tensor_scalar(cnti[:, :], cnts[:, :], 127.0, None, ALU.add))
            link(v.tensor_scalar(cntj[:, :], cnti[:, :], 7, None, ALU.arith_shift_right))
            link(v.tensor_copy(nch[:, :], cntj[:, :]))
            link(v.tensor_tensor_scan(ends[:, :], nch[:, :], g.zero[:, 0:NE], 0.0, ALU.add, ALU.add))
            link(v.tensor_tensor(begin[:, :], ends[:, :], nch[:, :], ALU.subtract))
            link(v.tensor_scalar(last[:, :], ends[:, NE - 1:NE], -1.0, None, ALU.add))
            link(v.tensor_scalar(chc[:, :], g.iota[:, 0:MC], last[:, 0:1], None, ALU.min))
            for q in range(NE - 1):
                v.tensor_scalar(past[:, q, :], chc[:, :], ends[:, q:q + 1], None, ALU.is_ge)
                ins = v.tensor_scalar(pastn[:, q, :], chc[:, :], ends[:, q:q + 1], nch[:, q:q + 1], ALU.is_ge, ALU.mult)
            link(ins)
            v.tensor_reduce(ex[:, :], past[:, :, :].rearrange("p q c -> p c q"), axis=AX.X, op=ALU.add)
            link(v.tensor_reduce(bg[:, :], pastn[:, :, :].rearrange("p q c -> p c q"), axis=AX.X, op=ALU.add))
            link(v.tensor_tensor(df[:, :], chc[:, :], bg[:, :], ALU.subtract))
            link(v.tensor_scalar(rw[:, :], df[:, :], 128.0, None, ALU.mult))
            v.scalar_tensor_tensor(g.chunk_row[:, :], ex[0:1, :], float(CAP), rw[0:1, :], ALU.mult, ALU.add)
            v.tensor_copy(g.chunk_expert[:, :], ex[0:1, :])


def expert_loop(nc, g):
    with ExitStack() as ctx:
        t = Parts(nc, ctx, "expert")
        sb, sem, sems = t.sb, t.sem, t.sems
        xs, xsT = sb("xs", [128, 2, D]), sb("xsT", [128, 2, 2, 128])
        b1bc, b2bc = sb("b1bc", [128, NE, HID]), sb("b2bc", [128, NE, D])
        hb, hg, hT = sb("hb", [128, 2, HID]), sb("hg", [128, 2, HID]), sb("hT", [128, 2, HID])
        meta, first_choice = sb("meta", [128, 2, XW - D]), sb("first_choice", [128, 2, 1])
        goal, goali = sb("goal", [128, 2, 2]), sb("goali", [128, 2, 1], I32)
        ysum, y = sb("ysum", [128, 2, D]), sb("y", [128, 2, D])
        yb_read = sem("yb_read")
        meta_in, goal_step = sems("meta_in", 2), sem("goal_step")
        b_in, xs_in, y_out = sem("b_in"), sems("xs_in", 2), sems("y_out", 2)
        xt_ready, xt_copied, h_ready, hb_ready = sem("ext_ready"), sem("ext_copied"), sem("eh_ready"), sem("hb_ready")
        hg_ready, ht_ready, ht_copied, y_made, y_ready = sem("hg_ready"), sem("ht_ready"), sem("ht_copied"), sem("y_made"), sem("y_ready")
        block = ctx.enter_context(nc.Block())
        b = g.bank
        XB, HB, TBK, YB = b[0:2], b[2:4], b[4:6], b[6:8]
        HALFC = MC // 2

        def experts(eng, j):
            first, last = isinstance(j, int) and j == 0, isinstance(j, int) and j == HALFC
            c0, n = (0 if first else 2 * j - 2), (2 if first or last else 4)
            _, e = nc.values_load_multi_w_load_instructions(g.chunk_expert[0:1, ds(c0, n)], engines=(eng.engine,),
                                                            min_val=0, max_val=NE - 1)
            return (None, None) * first + tuple(e)

        def pairs(eng, step):
            for j in range(2):
                step(j, experts(eng, j))
            with eng.Fori(2, HALFC - 1) as j:
                step(j, experts(eng, j))
            step(HALFC - 1, experts(eng, HALFC - 1))

        def wait(eng, sem, value):
            if not isinstance(value, int) or value > 0:
                eng.wait_ge(sem, value)

        def exists(c):
            return not isinstance(c, int) or 0 <= c < MC

        @block.sync
        def _(sp):
            sp.dma_start(b1bc[:, :, :], g.b1.rearrange("e h -> (e h)").partition_broadcast(128).rearrange("p (e h) -> p e h", e=NE)).then_inc(b_in, 16)
            sp.dma_start(b2bc[:, :, :], g.b2.rearrange("e h -> (e h)").partition_broadcast(128).rearrange("p (e h) -> p e h", e=NE)).then_inc(b_in, 16)

            def step(j, first):
                for k in range(2):
                    c = 2 * j + k
                    row = sp.value_load(g.chunk_row[0:1, ds(c, 1)], min_val=0, max_val=NE * CAP - 128)
                    if not first:
                        sp.wait_ge(xt_ready, c - 1)
                    sp.dma_start(xs[:, k, :], g.xs_d[ds(row, 128), 0:D]).then_inc(xs_in[k], 16)
            step(0, True)
            with sp.Fori(1, HALFC) as j:
                step(j, False)

        @block.gpsimd
        def _(pool):
            def fetch(c, k):
                row = pool.value_load(g.chunk_row[0:1, ds(c, 1)], min_val=0, max_val=NE * CAP - 128)
                pool.dma_start(meta[:, k, :], g.xs_d[ds(row, 128), D:XW]).then_inc(meta_in[k], 16)

            def store(c, j, k, first=False):
                if not (first and k == 0):
                    pool.wait_ge(y_out[1 - k], 16 * (j + k))
                after(pool, g, y_ready, c + 1)
                pool.indirect_dma_start(g.ys_d, bass.IndirectOffsetOnAxis(ap=goali[:, k, 0:1], axis=0), y[:, k, :], None).then_inc(y_out[k], 16)
            for k in range(2):
                fetch(k, k)
            for k in range(2):
                store(k, 0, k, True)
                fetch(2 + k, k)
            with pool.Fori(1, HALFC - 1) as j:
                for k in range(2):
                    store(2 * j + k, j, k)
                    fetch(2 * j + (2 + k), k)
            for k in range(2):
                store(MC - 2 + k, HALFC - 1, k)
            for k in range(2):
                pool.wait_ge(y_out[k], 16 * HALFC)

        @block.tensor
        def _(pe):
            def turn_x(c, k, use):
                pe.wait_ge(xs_in[k], 16 * use)
                wait(pe, xt_copied, c - 1)
                for q in range(2):
                    u = pe.transpose(XB[k][:, q * 128:(q + 1) * 128], xs[:, k, q * 128:(q + 1) * 128], g.ident)
                u.then_inc(xt_ready, 1)

            def hidden(c, k, e):
                pe.wait_ge(xt_copied, c + 1)
                wait(pe, hb_ready, c - 1)
                for q in range(2):
                    u = pe.matmul(HB[k][:, :], xsT[:, k, q, :], g.w1s[:, ds(e, 1), q, :].rearrange("p a f -> p (a f)"), start=(q == 0), stop=(q == 1))
                u.then_inc(h_ready, 1)

            def turn_h(c, k):
                pe.wait_ge(hg_ready, c + 1)
                wait(pe, ht_copied, c - 1)
                for q in range(4):
                    u = pe.transpose(TBK[k][:, q * 128:(q + 1) * 128], hg[:, k, q * 128:(q + 1) * 128], g.ident)
                u.then_inc(ht_ready, 1)

            def output(c, k, e):
                pe.wait_ge(ht_copied, c + 1)
                wait(pe, yb_read, c - 1)
                for q in range(4):
                    u = pe.matmul(YB[k][:, 0:D], hT[:, k, q * 128:(q + 1) * 128], g.w2s[:, ds(e, 1), q, :].rearrange("p a f -> p (a f)"), start=(q == 0), stop=(q == 3))
                u.then_inc(y_made, 1)

            def step(j, e):
                for k in range(2):
                    c = 2 * j + k
                    hidden(c, k, e[2 + k])
                    if exists(c + 1):
                        turn_x(c + 1, 1 - k, j + 1 + k)
                    if exists(c - 1):
                        turn_h(c - 1, 1 - k)
                    if exists(c - 2):
                        output(c - 2, k, e[k])
            turn_x(0, 0, 1)
            pairs(pe, step)
            e = experts(pe, HALFC)
            turn_h(MC - 1, 1)
            output(MC - 2, 0, e[0])
            output(MC - 1, 1, e[1])

        @block.scalar
        def _(act):
            def copy_x(c, k):
                act.wait_ge(xt_ready, c + 1)
                wait(act, h_ready, c - 1)
                act.copy(xsT[:, k, :, :], XB[k][:, 0:D].rearrange("p (q n) -> p q n", q=2)).then_inc(xt_copied, 1)

            def gelu(c, k):
                act.wait_ge(hb_ready, c + 1)
                wait(act, ht_ready, c - 1)
                act.activation(hg[:, k, :], hb[:, k, :], ACT.Gelu).then_inc(hg_ready, 1)

            def step(j):
                for k in range(2):
                    c = 2 * j + k
                    if exists(c + 1):
                        copy_x(c + 1, 1 - k)
                    gelu(c, k)
            copy_x(0, 0)
            for j in range(2):
                step(j)
            with act.Fori(2, HALFC - 1) as j:
                step(j)
            step(HALFC - 1)

        @block.vector
        def _(v):
            v.wait_ge(b_in, 32)

            def bias(c, k, e):
                v.wait_ge(h_ready, c + 1)
                wait(v, hg_ready, c - 1)
                v.tensor_tensor(hb[:, k, :], HB[k][:, :], b1bc[:, ds(e, 1), :].rearrange("p a f -> p (a f)"), ALU.add).then_inc(hb_ready, 1)

            def copy_h(c, k):
                v.wait_ge(ht_ready, c + 1)
                wait(v, y_made, c - 1)
                v.tensor_copy(hT[:, k, :], TBK[k][:, :]).then_inc(ht_copied, 1)

            def result(c, k, e, uses):
                v.wait_ge(meta_in[k], 16 * (uses + 1))
                wait(v, y_out[k], 16 * uses)
                v.tensor_tensor(first_choice[:, k, :], meta[:, k, C_E1 - D:XW - D], g.expert_of[:, ds(c, 1)], ALU.is_equal).then_inc(goal_step, 1)
                v.wait_ge(y_made, c + 1)
                v.tensor_tensor(ysum[:, k, :], YB[k][:, 0:D], b2bc[:, ds(e, 1), :].rearrange("p a f -> p (a f)"), ALU.add).then_inc(yb_read, 1)
                v.wait_ge(goal_step, 2 * c + 1)
                v.scalar_tensor_tensor(goal[:, k, :], meta[:, k, C_MN - D:C_E1 - D], first_choice[:, k, :], meta[:, k, 0:2],
                                       ALU.mult, ALU.add).then_inc(goal_step, 1)
                v.wait_ge(goal_step, 2 * c + 2)
                v.wait_ge(yb_read, c + 1)
                v.tensor_copy(goali[:, k, :], goal[:, k, 0:1])
                v.tensor_scalar(y[:, k, :], ysum[:, k, :], goal[:, k, 1:2], None, ALU.mult).then_inc(y_ready, 1)

            def step(j, e):
                for k in range(2):
                    c = 2 * j + k
                    bias(c, k, e[2 + k])
                    if exists(c - 1):
                        copy_h(c - 1, 1 - k)
                    if exists(c - 2):
                        result(c - 2, k, e[k], j - 1)
            pairs(v, step)
            e = experts(v, HALFC)
            copy_h(MC - 1, 1)
            result(MC - 2, 0, e[0], HALFC - 1)
            result(MC - 1, 1, e[1], HALFC - 1)


def combine(nc, g):
    with ExitStack() as ctx:
        t = Parts(nc, ctx, "combine")
        sb, sem, sems = t.sb, t.sem, t.sems
        PARTS = 10
        W = N * D // 128 // PARTS
        x2, y1, y2 = sb("cx2", [128, 3, W]), sb("cy1", [128, 3, W]), sb("cy2", [128, 3, W])
        o1, o2 = sb("o1", [128, 2, W]), sb("o2", [128, 3, W])
        x2_in, y1_in, y2_in, out_done = sems("x2_in", 3), sems("y1_in", 3), sems("y2_in", 3), sems("out_done", 3)
        o1_ready, o2_ready = sem("o1_ready"), sem("o2_ready")
        block = ctx.enter_context(nc.Block())

        def flat(ap, m):
            return ap.rearrange("n d -> (n d)").rearrange("(p w) -> p w", p=128)[:, m * W:(m + 1) * W]

        @block.sync
        def _(sp):
            for m in range(PARTS):
                if m >= 3:
                    sp.wait_ge(o2_ready, m - 2)
                sp.dma_start(x2[:, m % 3, :], flat(g.x2_d, m)).then_inc(x2_in[m % 3], 16)
                sp.dma_start(y1[:, m % 3, :], flat(g.ys_d[0:N, :], m)).then_inc(y1_in[m % 3], 16)

        @block.gpsimd
        def _(pool):
            for m in range(PARTS):
                if m >= 3:
                    pool.wait_ge(o2_ready, m - 2)
                pool.dma_start(y2[:, m % 3, :], flat(g.ys_d[N:2 * N, :], m)).then_inc(y2_in[m % 3], 16)

        @block.scalar
        def _(act):
            for m in range(PARTS):
                act.wait_ge(o2_ready, m + 1)
                act.dma_start(flat(g.out, m), o2[:, m % 3, :]).then_inc(out_done[m % 3], 16)
            for k in range(3):
                act.wait_ge(out_done[k], 16 * len(range(k, PARTS, 3)))

        @block.vector
        def _(v):
            for m in range(PARTS):
                r, use = m % 3, m // 3 + 1
                v.wait_ge(x2_in[r], 16 * use)
                v.wait_ge(y1_in[r], 16 * use)
                v.tensor_tensor(o1[:, m % 2, :], y1[:, r, :], x2[:, r, :], ALU.add).then_inc(o1_ready, 1)
                v.wait_ge(o1_ready, m + 1)
                v.wait_ge(y2_in[r], 16 * use)
                if m >= 3:
                    v.wait_ge(out_done[r], 16 * (use - 1))
                v.tensor_tensor(o2[:, r, :], y2[:, r, :], o1[:, m % 2, :], ALU.add).then_inc(o2_ready, 1)


class Shared:
    pass


def program(nc, ins, out):
    g = Shared()
    (g.x, g.src, g.dst, g.gW, g.gal, g.gar, g.wqkv, g.wout, g.bout, g.gamma, g.beta, g.wr, g.br,
     g.w1, g.b1, g.w2, g.b2, g.const) = ins
    g.out = out

    def dram(name, shape, dt=F32):
        return nc.dram_tensor(name, shape, dt, kind="Internal").ap()

    g.hist_d = dram("hist_d", (2, HI * LO))
    g.cols_d = dram("cols_d", (2, NB))
    g.sorted_d = dram("sorted_d", (128 * NCH, 1), I32)
    g.table_d = dram("table_d", (N, ROW))
    g.hl_d = dram("hl_d", (NB * BR, GH))
    g.sums_d = dram("sums_d", (NCH * BR, TW))
    g.node_d = dram("node_d", (NB * BR, 1), I32)
    g.x2_d = dram("x2_d", (N, D))
    g.xs_d = dram("xs_d", (NE * CAP, XW))
    g.ys_d = dram("ys_d", (2 * N + 128, D))
    with ExitStack() as ctx:
        t = Parts(nc, ctx, "all")
        sb = t.sb
        g.bank = [ctx.enter_context(nc.psum_tensor(f"bank{n}", [128, 512], F32)) for n in range(8)]
        g.late_in, g.filled = t.sem("late_in"), t.sem("filled")
        g.passed = t.sem("passed")
        g.cst = sb("cst", [128, CW])
        g.ident, g.iota = g.cst[:, C_ID:C_ID + 128], g.cst[:, C_IO:C_IO + NCH]
        g.ltb, g.geb = sb("ltb", [128, 128], BF16), sb("geb", [128, 128], BF16)
        g.iotab = sb("iotab", [128, NB], BF16)
        g.eps = sb("eps", [128, 1])
        g.ones, g.zero = sb("ones", [128, 128]), sb("zeros", [128, 512])

        g.wrs = sb("wrs", [128, 2, NE])
        g.w1s, g.w2s = sb("w1s", [128, NE, 2, HID]), sb("w2s", [128, NE, 4, D])
        g.nodeidx = sb("nodeidx", [TP, NT], I32)
        g.mixP = sb("mixP", [128, 2, D])
        g.expert_of = sb("expert_of", [128, MC])
        g.chunk_row, g.chunk_expert = sb("chunk_row", [1, MC], I32), sb("chunk_expert", [1, MC], I32)
        with ExitStack() as c2:
            t2 = Parts(nc, c2, "x")
            g.xnT = t2.sb("xnT", [128, NT, 2, TP])
            with ExitStack() as c3:
                t3 = Parts(nc, c3, "mix")
                g.woT, g.wq = t3.sb("woT", [128, 4, D]), t3.sb("wq", [128, 4, D])
                with ExitStack() as c4:
                    t4 = Parts(nc, c4, "node0")
                    g.wa = t4.sb("wa", [128, 2, D + 2 * GH])
                    g.wkvT = t4.sb("wkvT", [128, 2, 2 * INNER])
                    g.firsts = t4.sb("firsts", [128, 2, NB])
                    g.bktf, g.packi = t4.sb("bktf", [TP, EC]), t4.sb("packi", [TP, EC], I32)
                    setup(nc, g)
                    node_loop(nc, g)
                g.hlc, g.reset = t3.sb("hlc", [128, NCH]), t3.sb("reset", [128, NCH])
                g.local, g.colidx = t3.sb("local", [128, NCH]), t3.sb("colidx", [128, NCH], I32)
                chunk_tables(nc, g)
                edge_loop(nc, g)
            token_loop(nc, g)
        expert_loop(nc, g)
        combine(nc, g)


_INS = ["x", "src", "dst", "L0_gnn_W", "L0_gnn_a_l", "L0_gnn_a_r", "L0_mix_Wqkv", "L0_mix_Wout", "L0_mix_bout",
        "L0_ffn_gamma", "L0_ffn_beta", "L0_ffn_Wr", "L0_ffn_br", "L0_ffn_W1", "L0_ffn_b1", "L0_ffn_W2", "L0_ffn_b2"]


def kernel(**inputs):
    import numpy as np
    import concourse.bacc as bacc
    from concourse.bass_utils import run_bass_kernel_spmd

    nc = bacc.Bacc("TRN2", target_bir_lowering=False, num_devices=1)
    arrays = {f"in_{n}": np.ascontiguousarray(inputs[n]) for n in _INS}
    arrays["in_const"] = constants()
    ins = [nc.dram_tensor(n, a.shape, mybir.dt.from_np(a.dtype), kind="ExternalInput").ap() for n, a in arrays.items()]
    out = nc.dram_tensor("out", (N, D), F32, kind="ExternalOutput").ap()
    program(nc, ins, out)
    r = run_bass_kernel_spmd(nc, [arrays], core_ids=[0])
    return r.results[0]["out"]
```
